# Optimizing a Trainium2 kernel written in Bass

```python
import numpy as np
import jax
import jax.numpy as jnp

def _softmax(x, axis=-1):
    return jax.nn.softmax(x, axis=axis)

def _gelu(x):
    return jax.nn.gelu(x, approximate=True)

def _silu(x):
    return jax.nn.silu(x)

def _sigmoid(x):
    return jax.nn.sigmoid(x)

def _layernorm(x, axis=-1, eps=1e-05):
    m = jnp.mean(x, axis=axis, keepdims=True)
    v = jnp.var(x, axis=axis, keepdims=True)
    return (x - m) / jnp.sqrt(v + eps)

def _scatter_add(tgt, idx, src, axis=0):
    return tgt.at[idx].add(src)

def _segment_sum(src, seg, n):
    return jax.ops.segment_sum(src, seg, n)
kernel_name = 'mk_vit_tower_cls_d1_tok_img768_r4_c4f0d3'

def setup_inputs(seed: int=0):
    np.random.seed(seed)
    _w = jnp.asarray

    def _rec_inputs():
        import jax
        import jax.numpy as jnp
        _rk = jax.random.key(seed)
        x = -0.000147625 + 0.999875 * jax.random.normal(jax.random.fold_in(_rk, 1), (64, 3, 224, 224), jnp.float32)
        cls_tok = 0.02 * jax.random.normal(jax.random.fold_in(_rk, 5), (1, 1, 192), jnp.float32)
        return (x, cls_tok)
    x, cls_tok = _rec_inputs()

    def _L0_tok_setup():
        import jax, jax.numpy as jnp
        import numpy as np
        B, NM, EMB, P, HP = (64, 3, 192, 16, 14)
        T = HP * HP
        SEQ = T + 1
        RANK = 64
        NEW_EMB = EMB
        LN_EPS = 1e-05
        key = jax.random.key(seed)
        ks = jax.random.split(key, 8)
        scale = EMB ** (-0.5)
        x = jax.random.normal(ks[0], (B, 3, HP * P, HP * P), jnp.float32)
        conv_w = 0.02 * jax.random.normal(ks[1], (NM, EMB, 3 * P * P), jnp.float32)
        class_emb = 0.02 * jax.random.normal(ks[2], (NM, EMB), jnp.float32)
        pos_emb = 0.02 * jax.random.normal(ks[3], (NM, SEQ, EMB), jnp.float32)
        M_diag = jnp.ones((NM * EMB,), jnp.float32) / NM
        M_a = 0.1 * scale * jax.random.normal(ks[4], (NM * EMB, RANK), jnp.float32) / RANK
        M_b = 0.1 * scale * jax.random.normal(ks[5], (RANK, NEW_EMB), jnp.float32) / RANK
        ln_w = jnp.ones((NEW_EMB,), jnp.float32)
        ln_b = jnp.zeros((NEW_EMB,), jnp.float32)
        return dict(x=x, conv_w=conv_w, class_emb=class_emb, pos_emb=pos_emb, M_diag=M_diag, M_a=M_a, M_b=M_b, ln_w=ln_w, ln_b=ln_b)
    _L0_tok_all = _L0_tok_setup()
    _L0_tok_in = {k: v for k, v in _L0_tok_all.items() if k in ('conv_w', 'class_emb', 'pos_emb', 'M_diag', 'M_a', 'M_b', 'ln_w', 'ln_b')}
    del _L0_tok_all

    def _L0_attn_setup():
        import jax, jax.numpy as jnp
        import numpy as np
        from jax import lax
        B_SZ, L, D, N, R = (1, 1024, 192, 16, 48)

        def _soft_clamp(x, lo=0.0001, hi=10.0):
            center = (hi + lo) / 2.0
            half_range = (hi - lo) / 2.0
            return center + half_range * jnp.tanh((x - center) / half_range)
        key = jax.random.key(seed)
        ks = jax.random.split(key, 6)
        x = jax.random.normal(ks[0], (B_SZ, L, D), jnp.float32)
        A_log = jnp.log(jnp.broadcast_to(jnp.arange(1, N + 1, dtype=jnp.float32), (D, N)))
        D_param = jnp.ones((D,), jnp.float32)
        W_bc = jax.random.normal(ks[1], (D, 2 * N), jnp.float32) / np.sqrt(D).astype(np.float32)
        W_dt = jax.random.normal(ks[2], (D, R), jnp.float32) / np.sqrt(D).astype(np.float32)
        W_dtp = jax.random.normal(ks[3], (R, D), jnp.float32) / np.sqrt(R).astype(np.float32)
        dt = jax.random.uniform(ks[4], (D,), jnp.float32, 0.001, 0.1)
        dt = jnp.clip(dt, 0.0001)
        b_dt = dt + jnp.log(-jnp.expm1(-dt))
        rms_scale = jnp.ones((D,), jnp.float32)
        return {'x': x, 'A_log': A_log, 'D_param': D_param, 'W_bc': W_bc, 'W_dt': W_dt, 'W_dtp': W_dtp, 'b_dt': b_dt, 'rms_scale': rms_scale}
    _L0_attn_all = _L0_attn_setup()
    _L0_attn_in = {k: v for k, v in _L0_attn_all.items() if k in ('A_log', 'D_param', 'W_bc', 'W_dt', 'W_dtp', 'b_dt', 'rms_scale')}
    del _L0_attn_all

    def _L0_ffn_setup():
        import jax, jax.numpy as jnp
        import numpy as np
        H = 192
        R = 64
        E = 8
        B, S = (8, 512)
        key = jax.random.key(seed)
        ks = jax.random.split(key, 10)
        s_in = 1.0 / np.sqrt(H)
        s_r = 1.0 / np.sqrt(R)
        return {'x': jax.random.normal(ks[0], (B, S, H), dtype=jnp.float32), 'enc_w': jax.random.uniform(ks[1], (H, R), jnp.float32, -s_in, s_in), 'enc_b': jax.random.uniform(ks[2], (R,), jnp.float32, -s_in, s_in), 'sw_w': jax.random.uniform(ks[3], (R, E), jnp.float32, -s_r, s_r), 'sw_b': jax.random.uniform(ks[4], (E,), jnp.float32, -s_r, s_r), 'w1': jax.random.uniform(ks[5], (E, H, R), jnp.float32, -s_in, s_in), 'b1': jax.random.uniform(ks[6], (E, R), jnp.float32, -s_in, s_in), 'w2': jax.random.uniform(ks[7], (E, R, H), jnp.float32, -s_r, s_r), 'b2': jax.random.uniform(ks[8], (E, H), jnp.float32, -s_r, s_r)}
    _L0_ffn_all = _L0_ffn_setup()
    _L0_ffn_in = {k: v for k, v in _L0_ffn_all.items() if k in ('enc_w', 'enc_b', 'sw_w', 'sw_b', 'w1', 'b1', 'w2', 'b2')}
    del _L0_ffn_all
    return {'x': x, 'cls_tok': cls_tok, 'L0_tok_conv_w': _L0_tok_in['conv_w'], 'L0_tok_class_emb': _L0_tok_in['class_emb'], 'L0_tok_pos_emb': _L0_tok_in['pos_emb'], 'L0_tok_M_diag': _L0_tok_in['M_diag'], 'L0_tok_M_a': _L0_tok_in['M_a'], 'L0_tok_M_b': _L0_tok_in['M_b'], 'L0_tok_ln_w': _L0_tok_in['ln_w'], 'L0_tok_ln_b': _L0_tok_in['ln_b'], 'L0_attn_A_log': _L0_attn_in['A_log'], 'L0_attn_D_param': _L0_attn_in['D_param'], 'L0_attn_W_bc': _L0_attn_in['W_bc'], 'L0_attn_W_dt': _L0_attn_in['W_dt'], 'L0_attn_W_dtp': _L0_attn_in['W_dtp'], 'L0_attn_b_dt': _L0_attn_in['b_dt'], 'L0_attn_rms_scale': _L0_attn_in['rms_scale'], 'L0_ffn_enc_w': _L0_ffn_in['enc_w'], 'L0_ffn_enc_b': _L0_ffn_in['enc_b'], 'L0_ffn_sw_w': _L0_ffn_in['sw_w'], 'L0_ffn_sw_b': _L0_ffn_in['sw_b'], 'L0_ffn_w1': _L0_ffn_in['w1'], 'L0_ffn_b1': _L0_ffn_in['b1'], 'L0_ffn_w2': _L0_ffn_in['w2'], 'L0_ffn_b2': _L0_ffn_in['b2']}

def reference(x, cls_tok, L0_tok_conv_w, L0_tok_class_emb, L0_tok_pos_emb, L0_tok_M_diag, L0_tok_M_a, L0_tok_M_b, L0_tok_ln_w, L0_tok_ln_b, L0_attn_A_log, L0_attn_D_param, L0_attn_W_bc, L0_attn_W_dt, L0_attn_W_dtp, L0_attn_b_dt, L0_attn_rms_scale, L0_ffn_enc_w, L0_ffn_enc_b, L0_ffn_sw_w, L0_ffn_sw_b, L0_ffn_w1, L0_ffn_b1, L0_ffn_w2, L0_ffn_b2):
    import jax
    import jax.numpy as jnp

    def _L0_tok_ref(x, conv_w, class_emb, pos_emb, M_diag, M_a, M_b, ln_w, ln_b):
        import jax, jax.numpy as jnp
        import numpy as np
        B, NM, EMB, P, HP = (64, 3, 192, 16, 14)
        T = HP * HP
        SEQ = T + 1
        RANK = 64
        NEW_EMB = EMB
        LN_EPS = 1e-05
        b = x.shape[0]
        patches = x.reshape(b, 3, HP, P, HP, P).transpose(0, 2, 4, 1, 3, 5).reshape(b, T, 3 * P * P)
        feats = jnp.einsum('btp,mep->btme', patches, conv_w)
        cls = jnp.broadcast_to(class_emb[None, None], (b, 1, NM, EMB))
        feats = jnp.concatenate([cls, feats], axis=1)
        feats = feats + pos_emb.transpose(1, 0, 2)[None]
        diag_part = jnp.einsum('bsme,me->bse', feats, M_diag.reshape(NM, EMB))
        flat = feats.reshape(b, SEQ, NM * EMB)
        low_rank = flat @ M_a @ M_b
        y = diag_part + low_rank
        mu = y.mean(-1, keepdims=True)
        var = y.var(-1, keepdims=True)
        y = (y - mu) * jax.lax.rsqrt(var + LN_EPS) * ln_w + ln_b
        return y

    def _L0_attn_ref(x, A_log, D_param, W_bc, W_dt, W_dtp, b_dt, rms_scale):
        import jax, jax.numpy as jnp
        import numpy as np
        from jax import lax
        B_SZ, L, D, N, R = (1, 1024, 192, 16, 48)

        def _soft_clamp(x, lo=0.0001, hi=10.0):
            center = (hi + lo) / 2.0
            half_range = (hi - lo) / 2.0
            return center + half_range * jnp.tanh((x - center) / half_range)
        n = A_log.shape[1]
        A = -jnp.exp(A_log)
        bc = x @ W_bc
        B_sel, C_sel = (bc[..., :n], bc[..., n:])
        delta = jax.nn.softplus(x @ W_dt @ W_dtp + b_dt)
        delta = delta * lax.rsqrt(jnp.mean(delta * delta, axis=-1, keepdims=True) + 1e-06) * rms_scale
        delta = _soft_clamp(delta, 0.0001, 10.0)
        dE = delta[..., None]
        half = 0.5 * dE * A
        denom = 1.0 - half
        A_bar = (1.0 + half) / denom
        B_bar = jnp.sqrt(dE) * B_sel[:, :, None, :] / denom
        x_prev = jnp.concatenate([jnp.zeros_like(x[:, :1]), x[:, :-1]], axis=1)
        x_in = 0.5 * (x + x_prev)
        Bx = B_bar * x_in[..., None]

        def op(left, right):
            a_l, b_l = left
            a_r, b_r = right
            return (a_r * a_l, a_r * b_l + b_r)
        _, all_h = lax.associative_scan(op, (A_bar, Bx), axis=1)
        y = jnp.sum(C_sel[:, :, None, :] * all_h, axis=-1)
        return y + D_param * x

    def _L0_ffn_ref(x, enc_w, enc_b, sw_w, sw_b, w1, b1, w2, b2):
        import jax, jax.numpy as jnp
        import numpy as np
        H = 192
        R = 64
        E = 8
        B, S = (8, 512)
        b, s, d = x.shape
        xt = x.reshape(-1, d)
        x_enc = xt @ enc_w + enc_b
        route_prob = jax.nn.softmax(x_enc @ sw_w + sw_b, axis=-1)
        route_prob_max = jnp.max(route_prob, axis=-1)
        routes = jnp.argmax(route_prob, axis=-1)
        onehot = jax.nn.one_hot(routes, E, dtype=xt.dtype)
        h = jnp.einsum('td,edr->ter', xt, w1) + b1[None]
        h = jax.nn.gelu(h, approximate=False)
        h = h * onehot[..., None]
        out = jnp.einsum('ter,erd->td', h, w2) + onehot @ b2
        out = out * route_prob_max[:, None]
        return out.reshape(b, s, d)
    h = _L0_tok_ref(x, L0_tok_conv_w, L0_tok_class_emb, L0_tok_pos_emb, L0_tok_M_diag, L0_tok_M_a, L0_tok_M_b, L0_tok_ln_w, L0_tok_ln_b)
    h = jnp.concatenate([jnp.broadcast_to(cls_tok, (h.shape[0], 1, h.shape[2])), h], axis=1)
    h = h + _L0_attn_ref(_layernorm(h, axis=-1), L0_attn_A_log, L0_attn_D_param, L0_attn_W_bc, L0_attn_W_dt, L0_attn_W_dtp, L0_attn_b_dt, L0_attn_rms_scale)
    h = h + _L0_ffn_ref(_layernorm(h, axis=-1), L0_ffn_enc_w, L0_ffn_enc_b, L0_ffn_sw_w, L0_ffn_sw_b, L0_ffn_w1, L0_ffn_b1, L0_ffn_w2, L0_ffn_b2)
    return h

_drawn_inputs = setup_inputs


def setup_inputs(seed=0):
    import zlib

    import numpy as np

    out = dict(_drawn_inputs(seed))
    spreads = {'L0_tok_M_diag': (0.3333333432674408, 0.2),
     'L0_tok_ln_w': (1.0, 0.2),
     'L0_tok_ln_b': (0.0, 0.1),
     'L0_attn_D_param': (1.0, 0.2),
     'L0_attn_rms_scale': (1.0, 0.6)}
    factors = {'L0_tok_M_a': 64.0,
     'L0_tok_M_b': 64.0,
     'L0_ffn_enc_w': 3.352,
     'L0_ffn_enc_b': 8.0,
     'L0_ffn_sw_w': 3.322,
     'L0_ffn_sw_b': 5.948,
     'L0_ffn_w1': 3.504,
     'L0_ffn_b1': 8.0,
     'L0_ffn_w2': 3.295,
     'L0_ffn_b2': 8.0}
    for name, (base, spread) in spreads.items():
        noise = np.random.default_rng([zlib.crc32(name.encode()), seed]).standard_normal(out[name].shape)
        drawn = base * np.exp(spread * noise) if base else spread * noise
        out[name] = jnp.asarray(drawn.astype(out[name].dtype))
    for name, factor in factors.items():
        out[name] = (out[name] * factor).astype(out[name].dtype)
    return out
```

```python
import math

import concourse.bass as bass
from concourse import mybir
from contextlib import ExitStack

FP32 = mybir.dt.float32
BF16 = mybir.dt.bfloat16
ALU = mybir.AluOpType
ACT = mybir.ActivationFunctionType
AXIS = mybir.AxisListType

B, CH, IMG = 64, 3, 224
P, HP = 16, 14
D, N, R, NM = 192, 16, 48, 3
RANK, E, ER = 64, 8, 64
SEQ = HP * HP + 2
HT = SEQ // 2
PAIRS = B // 2
T = 2
DB = 64
K3 = D // DB
W = D + 2 * N
SEG = SEQ + 1
G = N // 2
BW = K3 * SEG
GW = 2 * BW
PH = P // 2
KR = CH * P
KP = 64 + KR
HC = E * ER // 128
MC = 2 * NM
LN_EPS = 1e-5
RMS_EPS = 1e-6
CLAMP_MID = (10.0 + 0.0001) / 2.0
CLAMP_HALF = (10.0 - 0.0001) / 2.0
MASK = float(2.0 ** 60)
ZEROS_LOADS = 5
ZEROS_FIRST = 12
ZEROS_ALL = ZEROS_FIRST + 2
FOLD_MIXED = 3 + MC
FOLD_SPREAD = FOLD_MIXED + 14
FOLD_ALL = FOLD_SPREAD + 6


class Signal:

    def __init__(self, sem, steps):
        self.sem, self.steps = sem, steps

    def at(self, pair, k=None):
        return self.sem, pair * self.steps + (self.steps if k is None else k)


def first(pair):
    return isinstance(pair, int) and pair == 0


def alive(pair):
    return not isinstance(pair, int) or 0 <= pair < PAIRS


def build_program(nc, x, cls_tok, conv_w, class_emb, pos_emb, M_diag, M_a, M_b, ln_w, ln_b, A_log, D_param,
                  W_bc, W_dt, W_dtp, b_dt, rms_scale, enc_w, enc_b, sw_w, sw_b, w1, b1, w2, b2,
                  ident, eye_split, state_pick, dot_pick, expert_mask, rank_desc, out):
    ctx = ExitStack()
    with ctx:
        def sb(name, shape, dt=FP32):
            return ctx.enter_context(nc.sbuf_tensor(name, shape, dt))

        def pb(name, shape, dt=FP32):
            return ctx.enter_context(nc.psum_tensor(name, shape, dt))

        def signal(name, steps):
            return Signal(ctx.enter_context(nc.semaphore(name)), steps)

        idn = sb("idn", [128, 128])
        idb = sb("idb", [128, 128], BF16)
        eps = sb("eps", [128, 4])
        pick = sb("pick", [3 * T * N, N, 128], BF16)
        dpick = sb("dpick", [3 * T * N, 128], BF16)
        emask = sb("emask", [DB + E, E * ER], BF16)
        desc = sb("desc", [HT, E])
        w_eff = sb("w_eff", [KP, PH, D])
        tok_bias = sb("tok_bias", [HT, 2, D])
        lnw = sb("lnw", [HT, 2, D])
        lnb = sb("lnb", [HT, 2, D])
        dpar = sb("dpar", [HT, 2, D])
        rms_t = sb("rms_t", [HT, D])
        bdt_t = sb("bdt_t", [HT, 2, D])
        wp = sb("wp", [128, K3, W])
        a_bias = sb("a_bias", [128, K3, N])
        w1_s = sb("w1_s", [128, K3, E * ER])
        wr = sb("wr", [128, K3, E])
        w2_s = sb("w2_s", [128, HC, D])
        b1_s = sb("b1_s", [128, HC])
        b2_s = sb("b2_s", [E, D])
        br_t = sb("br_t", [HT, E])
        x_img = sb("x_img", [KP, T, SEQ * P])
        y_tok = sb("y_tok", [HT, 4 * D])
        bn6 = sb("bn6", [HT, 4, 6])
        mv1 = sb("mv1", [HT, 4, 2])
        mv2 = sb("mv2", [HT, 4, 2])
        mv3 = sb("mv3", [HT, 4, 2])
        six_count = sb("six_count", [HT, 4])
        bn6b = sb("bn6b", [HT, 4, 6])
        bn6c = sb("bn6c", [HT, 4, 6])
        rs1 = sb("rs1", [HT, 2, 4])
        rs2 = sb("rs2", [HT, 2, 4])
        rs3 = sb("rs3", [HT, 2, 4])
        h_tok = sb("h_tok", [HT, 4 * D])
        xn = sb("xn", [HT, 4 * D])
        hres = sb("hres", [HT, 2, 4 * D])
        xnT = sb("xnT", [128, 3, SEG])
        xd = sb("xd", [HT, 4 * D])
        nx = sb("nx", [HT, 4 * D])
        ex = sb("ex", [HT, 4 * D])
        lnu = sb("lnu", [HT, 4 * D])
        rem = sb("rem", [HT, 4 * D])
        sp_t = xd
        ms = sb("ms", [HT, 3, 4])
        dn, lnd = ex, lnu
        bcq = sb("bcq", [HT, 2, 3, T * N])
        prod = sb("prod", [HT, 2, T * N])
        res1 = sb("res1", [HT, 2, 3, T * N])
        res2 = sb("res2", [HT, 2, 3, T * N])
        split = sb("split", [HT, 2, 3, 3, T * N], BF16)
        bT = sb("bT", [96, 2, SEG + 1], BF16)
        cT = sb("cT", [96, 2, SEG + 1], BF16)
        qT = sb("qT", [96, 2, SEG + 1], BF16)
        ldT = sb("ldT", [128, 3, SEQ])
        sqT = sb("sqT", [128, 3, SEQ])
        gT = sb("gT", [128, 3, SEG])
        v_buf = sb("v_buf", [128, 2, 1 + GW])
        z_buf = sb("z_buf", [128, 2, GW])
        a_ring = sb("a_ring", [128, G, GW])
        p_buf = sb("p_buf", [128, 2, GW])
        acc = sb("acc", [128, 2, BW])
        h2 = sb("h2", [HT, 4 * D])
        x2 = sb("x2", [HT, 4 * D])
        x2T = sb("x2T", [128, 3, SEQ])
        lg = sb("lg", [HT, 4, E])
        lmax = sb("lmax", [HT, 3, 4])
        oh = sb("oh", [HT, 4, E])
        rank = sb("rank", [HT, 4, E])
        er = sb("er", [HT, 4, E])
        pm = sb("pm", [HT, 2, 4])
        ohT = sb("ohT", [E, T * SEQ])
        miss = sb("miss", [DB + E, SEQ], BF16)
        hid = sb("hid", [128, HC, T * SEQ])
        o_t = x2
        ring = a_ring[:, :, :].rearrange("p g w -> p (g w)")
        conv_s = ring[0:96, 0:MC * 768].rearrange("p (k n) -> p k n", k=MC)
        m_full = ring[0:96, 4608:4608 + MC * D].rearrange("p (k n) -> p k n", k=MC)
        ma_s = ring[0:96, 5760:5760 + MC * RANK].rearrange("p (k n) -> p k n", k=MC)
        maT = ring[0:RANK, 6144:6144 + MC * 96].rearrange("p (k n) -> p k n", k=MC)
        mb_s = ring[0:RANK, 6720:6720 + D]
        md_s = ring[0:96, 6912:6912 + MC]
        eyes = ring[0:96, 6920:6920 + 2 * D].rearrange("p (k n) -> p k n", k=2)
        wdt_s = ring[:, 7304:7304 + 2 * R].rearrange("p (k n) -> p k n", k=2)
        wdtT = ring[0:R, 7400:7400 + D]
        wdtp_s = ring[0:R, 7592:7592 + D]
        enc_s = ring[:, 7784:7784 + 2 * ER].rearrange("p (k n) -> p k n", k=2)
        encT = ring[0:ER, 7912:7912 + D]
        sw_s = ring[0:ER, 8104:8104 + E]
        encb_s = ring[0:ER, 8112:8113]
        encb_r = ring[0:ER, 8120:8120 + HT]
        swb_s = ring[0:HT, 8220:8220 + E]
        alog_s = ring[:, 8228:8228 + K3 * N].rearrange("p (k n) -> p k n", k=K3)
        vflat = v_buf[:, :, :].rearrange("p k w -> p (k w)")
        pos_s = vflat[0:HT, 0:2 * NM * D].rearrange("p (j n) -> p j n", j=2)
        cls_s = z_buf[0:HT, :, :].rearrange("p k w -> p (k w)")[:, 0:NM * D]
        posT = p_buf[0:96, :, :].rearrange("p k w -> p (k w)")[:, 0:2 * MC * HT].rearrange(
            "p (j k t) -> p j k t", j=2, k=MC)

        b_ps = pb("b_ps", [128, 2, 512])
        c_ps = pb("c_ps", [128, 2, 512])
        front_ps = pb("front_ps", [128, 2, 512])
        back_ps = pb("back_ps", [128, 2, 512])
        fold_banks = (front_ps[:, 0, :], front_ps[:, 1, :], c_ps[:, 0, :], c_ps[:, 1, :])
        front_bf = front_ps[:, 0, :].bitcast(BF16)

        def tile(t, m):
            return t.rearrange("p (j k t d) -> p j t k d", j=2, k=K3, t=T)[:, m % 2, m // 2]

        def by_image(t):
            return t.rearrange("p (a t d) -> p t a d", a=2 * K3, t=T)

        def over_images(t):
            return t.rearrange("p j (k d) -> p (j k) d", k=K3).unsqueeze(1).broadcast_to([HT, T, 2 * K3, DB])

        weights_in = signal("weights_in", 0)
        zeros_set = signal("zeros_set", 0)
        fold_pe = signal("fold_pe", 0)
        fold_dve = signal("fold_dve", 0)
        consts_set = signal("consts_set", 0)
        x_in = [signal(f"x_in{t}", 2 * CH * 16) for t in range(T)]
        out_stored = signal("out_stored", 4 * 16)
        tokens_pe = signal("tokens_pe", 4)
        tok_stats = signal("tok_stats", 10)
        tok_rstd = signal("tok_rstd", 2)
        h_ready = signal("h_ready", 15)
        h_rstd = signal("h_rstd", 2)
        xn_ready = signal("xn_ready", 4)
        hres_ready = signal("hres_ready", 2)
        xnT_pe = signal("xnT_pe", 2)
        xnT_act = signal("xnT_act", 2)
        proj_pe = signal("proj_pe", 4)
        proj_dve = signal("proj_dve", 12)
        softplus_act = signal("softplus_act", 2)
        softplus_dve = signal("softplus_dve", 4)
        rms_act = signal("rms_act", 6)
        delta_dve = signal("delta_dve", 4)
        clamp_act = signal("clamp_act", 2)
        bc_pe = signal("bc_pe", 1)
        bc_dve = signal("bc_dve", 3)
        lnd_pe = signal("lnd_pe", 2)
        lnd_act = signal("lnd_act", 4)
        g_dve = signal("g_dve", 2)
        dot_pe = signal("dot_pe", 1)
        acc_dve = signal("acc_dve", 1)
        b_pe = signal("b_pe", G)
        c_pe = signal("c_pe", G)
        v_dve = signal("v_dve", G)
        z_pool = signal("z_pool", G)
        a_act = signal("a_act", 6 * G)
        scan_dve = signal("scan_dve", G)
        p_dve = signal("p_dve", G)
        y_pool = signal("y_pool", 2 * G)
        yT_pe = signal("yT_pe", 2)
        h2_dve = signal("h2_dve", 11)
        h2_rstd = signal("h2_rstd", 2)
        x2_dve = signal("x2_dve", 4)
        x2T_pe = signal("x2T_pe", 2)
        x2T_act = signal("x2T_act", 2)
        logit_pe = signal("logit_pe", 1)
        route_dve = signal("route_dve", 7)
        route_act = signal("route_act", 1)
        onehot_pe = signal("onehot_pe", 1)
        onehot_dve = signal("onehot_dve", 3)
        hid_pe = signal("hid_pe", HC * T)
        hid_act = signal("hid_act", HC * T)
        ffn_pe = signal("ffn_pe", 2)
        out_dve = signal("out_dve", 6)

        block = ctx.enter_context(nc.Block())
        x_v = x.rearrange("b c (h p) w -> b c p h w", p=P)
        out_v = out.rearrange("(q t) (j p) d -> q t p j d", t=T, j=2)
        SETUP_LOADS = []

        @block.sync
        def _(sp):
            n = [0]

            def load(dst, src, columns=False):
                sp.dma_start(dst, src, allow_slow_non_contiguous=columns).then_inc(weights_in.sem, 16)
                n[0] += 1

            def load_x(p, t):
                if not first(p):
                    sp.wait_ge(*tokens_pe.at(p - 1, 2 * t + 2))
                for half in range(2):
                    for c in range(CH):
                        row = 64 * half + P * c
                        dst = x_img[row:row + P, t, 2 * P:].rearrange("p (h w) -> p h w", h=HP)
                        sp.dma_start(dst[:, :, 0:IMG - PH * half], x_v[p * T + t, c, :, :, PH * half:]) \
                          .then_inc(x_in[t].sem, 16)

            def store(p):
                sp.wait_ge(*out_dve.at(p))
                for t in range(T):
                    for j in range(2):
                        sp.dma_start(out_v[p, t, :, j, :].rearrange("p (k d) -> p k d", k=K3),
                                     tile(o_t[:, :], 2 * t + j)).then_inc(out_stored.sem, 16)

            load(idn[:, :], ident)
            load(ma_s, M_a.rearrange("(k p) r -> p k r", p=96))
            load(mb_s, M_b)
            load(md_s, M_diag.rearrange("(k p) -> p k", p=96), columns=True)
            load(eyes, eye_split)
            load(conv_s, conv_w.rearrange("m (k p) n -> p (m k) n", p=96))
            sp.wait_ge(zeros_set.sem, ZEROS_LOADS)
            for t in range(T):
                load_x(0, t)
            load(pos_s[1:HT, 0, :].rearrange("p (m e) -> p m e", m=NM), pos_emb[:, 0:HT - 1, :].rearrange("m s e -> s m e"))
            load(pos_s[:, 1, :].rearrange("p (m e) -> p m e", m=NM), pos_emb[:, HT - 1:, :].rearrange("m s e -> s m e"))
            load(cls_s[1:2, :].rearrange("p (m e) -> p m e", m=NM), class_emb.rearrange("(o m) e -> o m e", o=1))
            load(wdt_s[:, 0, :], W_dt[0:128, :])
            load(wdt_s[0:DB, 1, :], W_dt[128:D, :])
            load(wdtp_s, W_dtp)
            load(enc_s[:, 0, :], enc_w[0:128, :])
            load(enc_s[0:DB, 1, :], enc_w[128:D, :])
            load(sw_s, sw_w)
            load(encb_s, enc_b.rearrange("(p o) -> p o", o=1), columns=True)
            load(swb_s, sw_b.partition_broadcast(HT))
            for t in range(T):
                rows = slice(t * DB, (t + 1) * DB)
                load(wp[rows, :, D:W], W_bc.rearrange("(k p) n -> p k n", k=K3))
                load(alog_s[rows, :, :], A_log.rearrange("(k p) n -> p k n", k=K3))
                for k in range(K3):
                    load(w1_s[rows, k, :].rearrange("d (e r) -> d e r", e=E),
                         w1[:, k * DB:(k + 1) * DB, :].rearrange("e d r -> d e r"))
            for j in range(2):
                load(lnw[j == 0:HT, j, :], ln_w.partition_broadcast(HT - (j == 0)))
                load(lnb[j == 0:HT, j, :], ln_b.partition_broadcast(HT - (j == 0)))
                load(dpar[:, j, :], D_param.partition_broadcast(HT))
                load(bdt_t[:, j, :], b_dt.partition_broadcast(HT))
            load(lnb[0:1, 0, :], cls_tok[0, :, :])
            load(rms_t[:, :], rms_scale.partition_broadcast(HT))
            load(w2_s[:, :, :], w2.rearrange("(c e) r d -> (e r) c d", e=2))
            load(b1_s[:, :], b1.rearrange("(c e) r -> (e r) c", e=2), columns=True)
            load(b2_s[:, :], b2)
            load(pick[:, :, :], state_pick.bitcast(BF16))
            load(dpick[:, :], dot_pick.bitcast(BF16))
            for t in range(T):
                load(emask[t * DB:t * DB + E, :], expert_mask.bitcast(BF16))
            load(desc[:, :], rank_desc)
            SETUP_LOADS.append(16 * n[0])
            def iteration(q):
                if alive(q - 2):
                    store(q - 2)
                for t in range(T):
                    if alive(q + 3):
                        load_x(q + 3, t)

            for q in (-2, -1, 0, 1):
                iteration(q)
            with sp.Fori(0, PAIRS - 5) as i:
                iteration(i + 2)
            for q in range(PAIRS - 3, PAIRS + 2):
                iteration(q)
            sp.wait_ge(*out_stored.at(PAIRS - 1))

        @block.gpsimd
        def _(pool):
            for view in (pos_s[0:1, 0, :], cls_s, lnw[0:1, 0, :], lnb[0:1, 0, :], x_img[:, :, :], w_eff[:, :, :],
                         xnT[:, :, 0:1], gT[:, :, 0:1], bT[:, :, :], cT[:, :, :], qT[:, :, :],
                         bcq[:, :, :, :]):
                nc.gpsimd.memset(view, 0.0).then_inc(zeros_set.sem, 1)
            pool.wait_ge(fold_dve.sem, FOLD_ALL)
            nc.gpsimd.memset(a_ring[:, :, :].rearrange("p g (k w) -> p (g k) w", w=SEG)[:, :, 0:1], 0.0) \
                .then_inc(zeros_set.sem, 1)
            nc.gpsimd.memset(v_buf[:, :, 0:1], 0.0).then_inc(zeros_set.sem, 1)

            def z_sum(q, g):
                pool.wait_ge(*v_dve.at(q, g + 1))
                if not (first(q) and g < 2):
                    pool.wait_ge(*scan_dve.at(q, g - 1))
                nc.gpsimd.tensor_tensor(z_buf[:, g % 2, :], v_buf[:, g % 2, 1:1 + GW], v_buf[:, g % 2, 0:GW], ALU.add) \
                    .then_inc(z_pool.sem, 1)

            def state_sum(q, g, par):
                pool.wait_ge(*p_dve.at(q, g + 1))
                pr = p_buf[:, g % 2, :]
                for u in range(2):
                    if not (first(q) and g == 0 and u == 0):
                        pool.wait_ge(*y_pool.at(q, 2 * g + u))
                    nc.gpsimd.tensor_tensor(acc[:, par, :], acc[:, par, :], p_buf[:, g % 2, u * BW:(u + 1) * BW],
                                            ALU.add).then_inc(y_pool.sem, 1)

            def residual(p, par):
                pool.wait_ge(*xn_ready.at(p))
                if not (isinstance(p, int) and p < 2):
                    pool.wait_ge(*h2_dve.at(p - 2, 2))
                nc.gpsimd.tensor_tensor(by_image(hres[:, par, :]), by_image(xn[:, :]), over_images(dpar[:, :, :]), ALU.mult) \
                    .then_inc(hres_ready.sem, 1)
                pool.wait_ge(*hres_ready.at(p, 1))
                nc.gpsimd.tensor_tensor(hres[:, par, :], hres[:, par, :], h_tok[:, :], ALU.add) \
                    .then_inc(hres_ready.sem, 1)

            def iteration(q, par):
                for g in range(G):
                    if alive(q) and g + 1 < G:
                        z_sum(q, g + 1)
                    if alive(q + 1) and g + 1 == G:
                        z_sum(q + 1, 0)
                    if alive(q):
                        state_sum(q, g, par)
                    if alive(q + 1) and g == 2:
                        residual(q + 1, 1 - par)

            for q in (-1, 0, 1):
                iteration(q, q % 2)
            with pool.Fori(0, (PAIRS - 4) // 2) as i:
                iteration(i * 2 + 2, 0)
                iteration(i * 2 + 3, 1)
            for q in range(PAIRS - 2, PAIRS):
                iteration(q, q % 2)

        @block.scalar
        def _(act):
            act.wait_ge(fold_dve.sem, FOLD_ALL)

            def rstd(p, stats, mv, rs, done):
                act.wait_ge(*stats.at(p))
                nc.scalar.activation(rs[:, 0, :], mv[:, :, 1], ACT.Ln, bias=eps[0:HT, 0:1]).then_inc(done.sem, 1)
                act.wait_ge(*done.at(p, 1))
                nc.scalar.activation(rs[:, 1, :], rs[:, 0, :], ACT.Exp, scale=-0.5).then_inc(done.sem, 1)

            def xnT_copy(p):
                if not first(p):
                    act.wait_ge(*g_dve.at(p - 1))
                act.wait_ge(*xnT_pe.at(p))
                nc.scalar.activation(xnT[:, 0:2, 1:], front_ps[:, 0, 0:2 * SEQ].rearrange("p (k w) -> p k w", k=2),
                                     ACT.Copy).then_inc(xnT_act.sem, 1)
                nc.scalar.activation(xnT[:, 2, 1:], front_ps[:, 1, 0:SEQ], ACT.Copy).then_inc(xnT_act.sem, 1)

            def softplus(p):
                act.wait_ge(*proj_dve.at(p, 5))
                nc.scalar.activation(ex[:, :], nx[:, :], ACT.Exp).then_inc(softplus_act.sem, 1)
                act.wait_ge(*softplus_act.at(p, 1))
                nc.scalar.activation(lnu[:, :], ex[:, :], ACT.Ln, bias=1.0).then_inc(softplus_act.sem, 1)

            def rms(p):
                act.wait_ge(*softplus_dve.at(p))
                for m in range(4):
                    nc.scalar.activation(tile(rem[:, :], m), tile(sp_t[:, :], m), ACT.Square, accum_out=ms[:, 0, m:m + 1]) \
                        .then_inc(rms_act.sem, 1)
                act.wait_ge(*rms_act.at(p, 4))
                nc.scalar.activation(ms[:, 1, :], ms[:, 0, :], ACT.Ln, scale=1.0 / D, bias=eps[0:HT, 1:2]) \
                    .then_inc(rms_act.sem, 1)
                act.wait_ge(*rms_act.at(p, 5))
                nc.scalar.activation(ms[:, 2, :], ms[:, 1, :], ACT.Exp, scale=-0.5).then_inc(rms_act.sem, 1)

            def clamp(p):
                act.wait_ge(*delta_dve.at(p))
                nc.scalar.activation(nx[:, :], dn[:, :], ACT.Tanh, scale=1.0 / CLAMP_HALF, bias=eps[0:HT, 2:3]) \
                    .then_inc(clamp_act.sem, 1)
                nc.scalar.preload_act_table_set("natural_log_exp_and_others")
                act.wait_ge(*clamp_act.at(p, 1))
                nc.scalar.activation(lnd[:, :], nx[:, :], ACT.Ln, scale=CLAMP_HALF, bias=eps[0:HT, 3:4]) \
                    .then_inc(clamp_act.sem, 1)

            def lnd_copy(p):
                act.wait_ge(*lnd_pe.at(p))
                if not first(p):
                    act.wait_ge(*a_act.at(p - 1))
                ab = front_ps[:, 0, 0:2 * SEQ].rearrange("p (k w) -> p k w", k=2)
                tail = front_ps[:, 1, 0:SEQ]
                nc.scalar.activation(sqT[:, 0:2, :], ab, ACT.Exp, scale=0.5).then_inc(lnd_act.sem, 1)
                nc.scalar.activation(sqT[:, 2, :], tail, ACT.Exp, scale=0.5).then_inc(lnd_act.sem, 1)
                nc.scalar.activation(ldT[:, 0:2, :], ab, ACT.Copy).then_inc(lnd_act.sem, 1)
                nc.scalar.activation(ldT[:, 2, :], tail, ACT.Copy).then_inc(lnd_act.sem, 1)

            def decays(p, g):
                if g == 0:
                    act.wait_ge(*lnd_act.at(p))
                if not first(p):
                    act.wait_ge(*scan_dve.at(p - 1, g + 1))
                for u in range(2):
                    for k in range(K3):
                        col = (u * K3 + k) * SEG
                        nc.scalar.activation(a_ring[:, g, col + 1:col + SEG], ldT[:, k, :], ACT.Tanh, scale=-0.5,
                                             bias=a_bias[:, k, 2 * g + u:2 * g + u + 1]).then_inc(a_act.sem, 1)

            def x2T_copy(p):
                act.wait_ge(*x2T_pe.at(p))
                nc.scalar.activation(x2T[:, 0:2, :], back_ps[:, 0, 0:2 * SEQ].rearrange("p (k w) -> p k w", k=2),
                                     ACT.Copy).then_inc(x2T_act.sem, 1)
                nc.scalar.activation(x2T[:, 2, :], back_ps[:, 1, 0:SEQ], ACT.Copy).then_inc(x2T_act.sem, 1)

            def route_exp(p):
                act.wait_ge(*route_dve.at(p))
                nc.scalar.activation(er[:, :, :], lg[:, :, :], ACT.Exp).then_inc(route_act.sem, 1)

            def hidden(p, c, t):
                act.wait_ge(*hid_pe.at(p, T * c + t + 1))
                nc.scalar.activation(hid[:, c, t * SEQ:(t + 1) * SEQ], back_ps[:, t, 0:SEQ], ACT.Gelu,
                                     bias=b1_s[:, c:c + 1]).then_inc(hid_act.sem, 1)

            def iteration(q):
                scan, front, tok, back = (alive(q + o) for o in (0, 1, 2, -1))
                nc.scalar.preload_act_table_set("natural_log_exp_and_others")
                if front:
                    softplus(q + 1)
                if back:
                    rstd(q - 1, h2_dve, mv3, rs3, h2_rstd)
                if front:
                    rms(q + 1)
                nc.scalar.preload_act_table_set("gelu_and_others")
                if front:
                    clamp(q + 1)
                if back:
                    x2T_copy(q - 1)
                if tok:
                    rstd(q + 2, tok_stats, mv1, rs1, tok_rstd)
                if front:
                    lnd_copy(q + 1)
                if back:
                    route_exp(q - 1)
                if tok:
                    rstd(q + 2, h_ready, mv2, rs2, h_rstd)
                nc.scalar.preload_act_table_set("gelu_and_others")
                for g in range(G):
                    if front:
                        decays(q + 1, g)
                    if back:
                        hidden(q - 1, g // T, g % T)
                    if tok and g == 5:
                        xnT_copy(q + 2)

            for q in (-2, -1, 0, 1):
                iteration(q)
            with act.Fori(0, (PAIRS - 4) // 2) as i:
                iteration(i * 2 + 2)
                iteration(i * 2 + 3)
            for q in range(PAIRS - 2, PAIRS + 1):
                iteration(q)

        @block.tensor
        def _(pe):
            pe.wait_ge(weights_in.sem, SETUP_LOADS[0])
            pe.wait_ge(zeros_set.sem, ZEROS_FIRST)
            pe.wait_ge(fold_dve.sem, 1)
            for k in range(MC):
                last = nc.tensor.transpose(front_ps[0:RANK, k // 4, (k % 4) * 96:(k % 4 + 1) * 96], ma_s[:, k, :],
                                           idn[0:96, 0:96])
            last.then_inc(fold_pe.sem, 1)
            pe.wait_ge(fold_dve.sem, 3)
            for k in range(MC):
                bank = back_ps[:, k // 2, :] if k < 4 else b_ps[:, 0, :]
                last = nc.tensor.matmul(bank[0:96, (k % 2) * D:(k % 2 + 1) * D], maT[:, k, :], mb_s,
                                        start=True, stop=True)
            last.then_inc(fold_pe.sem, 1)
            pe.wait_ge(fold_dve.sem, FOLD_MIXED)
            pixels = conv_s.rearrange("p k (r x) -> p k x r", x=P)
            for px in range(P):
                half, col = px // PH, px % PH
                for k in range(MC):
                    last = nc.tensor.matmul(fold_banks[col // 2][64 * half:64 * half + KR, (col % 2) * D:(col % 2 + 1) * D],
                                            pixels[:, k, px, :], m_full[:, k, :], start=k == 0, stop=k == MC - 1)
            for jk in range(2 * MC):
                bank = (back_ps[:, 0, :], back_ps[:, 1, :], b_ps[:, 0, :])[jk // 4]
                last = nc.tensor.transpose(bank[0:96, (jk % 4) * HT:(jk % 4 + 1) * HT],
                                           pos_s[:, jk // MC, (jk % MC) * 96:(jk % MC + 1) * 96], idn[0:HT, 0:HT])
            for c, (w, cols) in enumerate(((wdt_s, R), (enc_s, ER))):
                nc.tensor.transpose(b_ps[0:cols, 1, c * D:c * D + 128], w[:, 0, :], idn[:, :])
                last = nc.tensor.transpose(b_ps[0:cols, 1, c * D + 128:(c + 1) * D], w[0:DB, 1, :], idn[0:DB, 0:DB])
            last.then_inc(fold_pe.sem, 1)
            pe.wait_ge(fold_dve.sem, FOLD_SPREAD)
            for j in range(2):
                for k in range(MC):
                    nc.tensor.matmul(back_ps[0:HT, 0, j * D:(j + 1) * D], posT[:, j, k, :], m_full[:, k, :],
                                     start=k == 0, stop=k == MC - 1)
            for k in range(K3):
                for t in range(T):
                    rows, cols = slice(t * DB, (t + 1) * DB), slice(k * DB, (k + 1) * DB)
                    nc.tensor.matmul(front_ps[rows, k // 2, (k % 2) * D:(k % 2 + 1) * D], wdtT[:, cols], wdtp_s,
                                     start=True, stop=True)
                    nc.tensor.matmul(back_ps[rows, 1, k * E:(k + 1) * E], encT[:, cols], sw_s, start=True, stop=True)
            nc.tensor.matmul(b_ps[0:HT, 0, 0:E], encb_r, sw_s, start=True, stop=True).then_inc(fold_pe.sem, 1)
            pe.wait_ge(fold_dve.sem, FOLD_ALL)

            def tokens(p, m):
                t, j = m // 2, m % 2
                if j == 0:
                    pe.wait_ge(*x_in[t].at(p))
                if m == 0 and not first(p):
                    pe.wait_ge(*proj_dve.at(p - 1, 4))
                for px in range(PH):
                    pixels = x_img[:, t, j * HT * P:(j + 1) * HT * P].rearrange("p (s x) -> p x s", x=P)
                    last = nc.tensor.matmul(front_ps[0:HT, t, j * D:(j + 1) * D], pixels[:, px, :], w_eff[:, px, :],
                                            start=px == 0, stop=px == PH - 1)
                last.then_inc(tokens_pe.sem, 1)

            def to_channels(src, dst, done):
                for k in range(K3):
                    for j in range(2):
                        col = j * T * D + k * 128
                        last = nc.tensor.transpose(dst[:, k // 2, (k % 2) * SEQ + j * HT:(k % 2) * SEQ + (j + 1) * HT],
                                                   src[:, col:col + 128], idn[0:HT, 0:HT])
                    if k:
                        last.then_inc(done.sem, 1)

            def xn_transpose(p):
                pe.wait_ge(*xn_ready.at(p))
                if not first(p):
                    pe.wait_ge(*lnd_act.at(p - 1))
                to_channels(xn, front_ps, xnT_pe)

            def project(p, m):
                if m == 0:
                    pe.wait_ge(*xnT_act.at(p))
                t, j = m // 2, m % 2
                rows, cols = slice(t * DB, (t + 1) * DB), slice(1 + j * HT, 1 + (j + 1) * HT)
                for k in range(K3):
                    last = nc.tensor.matmul(front_ps[0:HT, t, j * W:(j + 1) * W], xnT[rows, k, cols], wp[rows, k, :],
                                            start=k == 0, stop=k == K3 - 1)
                last.then_inc(proj_pe.sem, 1)

            def bc_transpose(p):
                pe.wait_ge(*proj_dve.at(p))
                if alive(p + 1):
                    pe.wait_ge(*tok_stats.at(p + 1, 1))
                for j in range(2):
                    for k in range(3):
                        last = nc.tensor.transpose(front_bf[0:96, k * 256 + j * 100:k * 256 + j * 100 + HT],
                                                   split[:, j, k, :, :].rearrange("p s n -> p (s n)"), idb[0:HT, 0:HT])
                last.then_inc(bc_pe.sem, 1)

            def lnd_transpose(p):
                pe.wait_ge(*clamp_act.at(p))
                pe.wait_ge(*bc_dve.at(p))
                to_channels(lnd, front_ps, lnd_pe)

            def dot_fill(q, par):
                pe.wait_ge(*bc_dve.at(q))
                nc.tensor.matmul(b_ps[:, 0, 0:SEG], dpick[:, :], qT[:, par, 0:SEG], start=True, stop=True) \
                    .then_inc(dot_pe.sem, 1)

            def group_fill(bank, rows, g, par):
                for u in range(2):
                    last = nc.tensor.matmul(bank[:, u * SEG:(u + 1) * SEG], pick[:, 2 * g + u, :], rows[:, par, 0:SEG],
                                            start=True, stop=True)
                return last

            def b_fill(q, g, par):
                if g == 0:
                    pe.wait_ge(*acc_dve.at(q))
                elif g >= 2:
                    pe.wait_ge(*v_dve.at(q, g - 1))
                group_fill(b_ps[:, g % 2, :], bT, g, par).then_inc(b_pe.sem, 1)

            def c_fill(q, g, par):
                if not (first(q) and g < 2):
                    pe.wait_ge(*p_dve.at(q, g - 1))
                group_fill(c_ps[:, g % 2, :], cT, g, par).then_inc(c_pe.sem, 1)

            def y_transpose(p, par):
                pe.wait_ge(*y_pool.at(p))
                if not first(p):
                    pe.wait_ge(*out_dve.at(p - 1))
                for j in range(2):
                    for k in range(K3):
                        last = nc.tensor.transpose(back_ps[0:HT, j, k * 128:(k + 1) * 128],
                                                   acc[:, par, k * SEG + 1 + j * HT:k * SEG + 1 + (j + 1) * HT], idn[:, :])
                    last.then_inc(yT_pe.sem, 1)

            def x2_transpose(p):
                pe.wait_ge(*x2_dve.at(p))
                to_channels(x2, back_ps, x2T_pe)

            def logits(p):
                pe.wait_ge(*x2T_act.at(p))
                for m in range(4):
                    rows, cols = slice((m // 2) * DB, (m // 2 + 1) * DB), slice((m % 2) * HT, (m % 2 + 1) * HT)
                    for k in range(K3):
                        last = nc.tensor.matmul(back_ps[0:HT, m // 2, (m % 2) * E:(m % 2 + 1) * E], x2T[rows, k, cols], wr[rows, k, :],
                                                start=k == 0, stop=k == K3 - 1)
                last.then_inc(logit_pe.sem, 1)

            def onehot_transpose(p):
                pe.wait_ge(*route_dve.at(p))
                for m in range(4):
                    last = nc.tensor.transpose(back_ps[0:E, 1, m * HT:(m + 1) * HT], oh[:, m, :], idn[0:HT, 0:HT])
                last.then_inc(onehot_pe.sem, 1)

            def hidden(p, c):
                cols = slice(c * 128, (c + 1) * 128)
                for t in range(T):
                    if c == 0:
                        pe.wait_ge(*onehot_dve.at(p))
                    else:
                        pe.wait_ge(*hid_act.at(p, T * (c - 1) + t + 1))
                    o, rows = back_ps[:, t, 0:SEQ], slice(t * DB, (t + 1) * DB)
                    for k in range(K3):
                        nc.tensor.matmul(o, w1_s[rows, k, cols], x2T[rows, k, :], start=k == 0, stop=False)
                    rows = slice(t * DB, t * DB + E)
                    nc.tensor.matmul(o, emask[rows, cols], miss[rows, :], start=False, stop=True) \
                        .then_inc(hid_pe.sem, 1)

            def experts(p, m):
                if m == 0:
                    pe.wait_ge(*hid_act.at(p))
                o = back_ps[0:HT, m // 2, (m % 2) * D:(m % 2 + 1) * D]
                cols = slice(m * HT, (m + 1) * HT)
                for c in range(HC):
                    nc.tensor.matmul(o, hid[:, c, cols], w2_s[:, c, :], start=c == 0, stop=False)
                last = nc.tensor.matmul(o, ohT[:, cols], b2_s[:, :], start=False, stop=True)
                if m % 2:
                    last.then_inc(ffn_pe.sem, 1)

            def iteration(q, par):
                scan, front, tok, back, last = (alive(q + o) for o in (0, 1, 2, -1, -2))

                def fills(g):
                    if scan and g + 2 < G:
                        b_fill(q, g + 2, par)
                    if scan and g + 1 < G:
                        c_fill(q, g + 1, par)

                fills(0)
                if front:
                    project(q + 1, 0)
                    project(q + 1, 1)
                    project(q + 1, 2)
                    project(q + 1, 3)
                fills(1)
                if last:
                    for m in range(4):
                        experts(q - 2, m)
                fills(2)
                if back:
                    y_transpose(q - 1, 1 - par)
                if tok:
                    tokens(q + 2, 0)
                    tokens(q + 2, 1)
                fills(3)
                if tok:
                    tokens(q + 2, 2)
                    tokens(q + 2, 3)
                if back:
                    x2_transpose(q - 1)
                fills(4)
                if back:
                    logits(q - 1)
                if front:
                    bc_transpose(q + 1)
                    lnd_transpose(q + 1)
                fills(5)
                if back:
                    onehot_transpose(q - 1)
                    hidden(q - 1, 0)
                fills(6)
                if front:
                    dot_fill(q + 1, 1 - par)
                if back:
                    hidden(q - 1, 1)
                if tok:
                    xn_transpose(q + 2)
                if front:
                    b_fill(q + 1, 0, 1 - par)
                    b_fill(q + 1, 1, 1 - par)
                    c_fill(q + 1, 0, 1 - par)
                if back:
                    hidden(q - 1, 2)
                    hidden(q - 1, 3)

            for q in (-2, -1, 0, 1):
                iteration(q, q % 2)
            with pe.Fori(0, (PAIRS - 4) // 2) as i:
                iteration(i * 2 + 2, 0)
                iteration(i * 2 + 3, 1)
            for q in range(PAIRS - 2, PAIRS + 2):
                iteration(q, q % 2)

        @block.vector
        def _(dve):
            v = nc.vector
            dve.wait_ge(weights_in.sem, SETUP_LOADS[0])
            dve.wait_ge(zeros_set.sem, ZEROS_FIRST)
            v.memset(eps[:, 0:1], LN_EPS).then_inc(consts_set.sem, 1)
            v.memset(eps[:, 1:2], RMS_EPS).then_inc(consts_set.sem, 1)
            v.memset(eps[:, 2:3], -CLAMP_MID / CLAMP_HALF).then_inc(consts_set.sem, 1)
            v.memset(eps[:, 3:4], CLAMP_MID).then_inc(consts_set.sem, 1)
            v.tensor_copy(idb[:, :], idn[:, :]).then_inc(consts_set.sem, 1)
            v.tensor_tensor(pos_s[:, 0, :], pos_s[:, 0, :], cls_s, ALU.add).then_inc(fold_dve.sem, 1)
            dve.wait_ge(fold_pe.sem, 1)
            v.tensor_copy(maT[:, 0:4, :], front_ps[0:RANK, 0, 0:4 * 96].rearrange("p (k n) -> p k n", k=4)) \
                .then_inc(fold_dve.sem, 1)
            v.tensor_copy(maT[:, 4:6, :], front_ps[0:RANK, 1, 0:2 * 96].rearrange("p (k n) -> p k n", k=2)) \
                .then_inc(fold_dve.sem, 1)
            dve.wait_ge(fold_pe.sem, 2)
            for k in range(MC):
                bank = back_ps[:, k // 2, :] if k < 4 else b_ps[:, 0, :]
                v.scalar_tensor_tensor(m_full[:, k, :], eyes[:, k % 2, :], md_s[:, k:k + 1],
                                       bank[0:96, (k % 2) * D:(k % 2 + 1) * D], ALU.mult, ALU.add) \
                    .then_inc(fold_dve.sem, 1)
            dve.wait_ge(fold_pe.sem, 3)
            for b, bank in enumerate(fold_banks):
                for rows in (slice(0, KR), slice(64, KP)):
                    v.tensor_copy(w_eff[rows, 2 * b:2 * b + 2, :],
                                  bank[rows, 0:2 * D].rearrange("p (k n) -> p k n", k=2)).then_inc(fold_dve.sem, 1)
            flat = posT.rearrange("p j k t -> p (j k t)")
            for b, bank in enumerate((back_ps[:, 0, :], back_ps[:, 1, :], b_ps[:, 0, :])):
                v.tensor_copy(flat[:, b * 4 * HT:(b + 1) * 4 * HT], bank[0:96, 0:4 * HT]).then_inc(fold_dve.sem, 1)
            v.tensor_copy(wdtT, b_ps[0:R, 1, 0:D]).then_inc(fold_dve.sem, 1)
            v.tensor_copy(encT, b_ps[0:ER, 1, D:2 * D]).then_inc(fold_dve.sem, 1)
            v.tensor_copy(encb_r, encb_s.broadcast_to([ER, HT])).then_inc(fold_dve.sem, 1)
            dve.wait_ge(fold_pe.sem, 4)
            v.tensor_copy(wp[:, 0:2, 0:D], front_ps[:, 0, 0:2 * D].rearrange("p (k n) -> p k n", k=2)) \
                .then_inc(fold_dve.sem, 1)
            v.tensor_copy(wp[:, 2, 0:D], front_ps[:, 1, 0:D]).then_inc(fold_dve.sem, 1)
            v.tensor_copy(wr[:, :, :], back_ps[:, 1, 0:K3 * E].rearrange("p (k e) -> p k e", k=K3)) \
                .then_inc(fold_dve.sem, 1)
            v.tensor_tensor(br_t[:, :], swb_s, b_ps[0:HT, 0, 0:E], ALU.add).then_inc(fold_dve.sem, 1)
            v.tensor_copy(tok_bias[:, :, :], back_ps[0:HT, 0, 0:2 * D].rearrange("p (j d) -> p j d", j=2)) \
                .then_inc(fold_dve.sem, 1)
            v.tensor_scalar(a_bias[:, :, :], alog_s, -0.5, 0.5 * math.log(2.0), ALU.mult, ALU.add) \
                .then_inc(fold_dve.sem, 1)
            dve.wait_ge(fold_dve.sem, FOLD_ALL)
            dve.wait_ge(zeros_set.sem, ZEROS_ALL)

            def over_tiles(t, width):
                return t.unsqueeze(1).broadcast_to([HT, 4, width])

            def statistics(p, src, six, mv, done, base):
                for m in range(4):
                    v.bn_stats(six[:, m, :], tile(src[:, :], m)).then_inc(done.sem, 1)
                dve.wait_ge(*done.at(p, base + 4))
                v.tensor_copy(six_count[:, :], six[:, :, 0]).then_inc(done.sem, 1)
                for m in range(4):
                    v.bn_aggr(mv[:, m, :], six[:, m, :]).then_inc(done.sem, 1)

            def normalise(dst, src, mv, rs, done):
                for m in range(4):
                    v.tensor_scalar(tile(dst[:, :], m), tile(src[:, :], m), mv[:, m, 0:1], rs[:, 1, m:m + 1],
                                    ALU.subtract, ALU.mult).then_inc(done.sem, 1)

            def tok_1(p):
                dve.wait_ge(*tokens_pe.at(p))
                v.tensor_tensor(by_image(y_tok[:, :]),
                                front_ps[0:HT, :, 0:2 * D].rearrange("p t (a d) -> p t a d", a=2 * K3),
                                over_images(tok_bias[:, :, :]), ALU.add).then_inc(tok_stats.sem, 1)
                dve.wait_ge(*tok_stats.at(p, 1))
                statistics(p, y_tok, bn6, mv1, tok_stats, 1)

            def tok_2(p):
                dve.wait_ge(*tok_rstd.at(p))
                if not first(p):
                    dve.wait_ge(*hres_ready.at(p - 1))
                normalise(h_tok, y_tok, mv1, rs1, h_ready)
                dve.wait_ge(*h_ready.at(p, 4))
                v.tensor_tensor(by_image(h_tok[:, :]), by_image(h_tok[:, :]), over_images(lnw[:, :, :]), ALU.mult).then_inc(h_ready.sem, 1)
                dve.wait_ge(*h_ready.at(p, 5))
                v.tensor_tensor(by_image(h_tok[:, :]), by_image(h_tok[:, :]), over_images(lnb[:, :, :]), ALU.add).then_inc(h_ready.sem, 1)
                dve.wait_ge(*h_ready.at(p, 6))
                statistics(p, h_tok, bn6b, mv2, h_ready, 6)

            def tok_3(p):
                dve.wait_ge(*h_rstd.at(p))
                if not first(p):
                    dve.wait_ge(*xnT_pe.at(p - 1))
                    dve.wait_ge(*hres_ready.at(p - 1))
                normalise(xn, h_tok, mv2, rs2, xn_ready)

            def proj_1(p):
                dve.wait_ge(*proj_pe.at(p))
                wide = front_ps[0:HT, :, 0:2 * W].rearrange("p t (j w) -> p t j w", j=2)
                for t in range(T):
                    v.tensor_tensor(xd[:, :].rearrange("p (j k t d) -> p t j k d", j=2, k=K3, t=T)[:, t],
                                    wide[:, t, :, 0:D].rearrange("p j (k d) -> p j k d", k=K3),
                                    bdt_t[:, :, :].rearrange("p j (k d) -> p j k d", k=K3), ALU.add) \
                        .then_inc(proj_dve.sem, 1)
                for k in range(2):
                    v.tensor_copy(bcq[:, :, k, :].rearrange("p j (t n) -> p t j n", t=T),
                                  wide[:, :, :, D + N * k:D + N * (k + 1)]).then_inc(proj_dve.sem, 1)
                dve.wait_ge(*proj_dve.at(p, 2))
                v.scalar_tensor_tensor(nx[:, :], xd[:, :], -1.0, xd[:, :], ALU.mult, ALU.min).then_inc(proj_dve.sem, 1)
                dve.wait_ge(*proj_dve.at(p, 4))
                v.tensor_tensor(prod[:, :, :], bcq[:, :, 0, :], bcq[:, :, 1, :], ALU.mult).then_inc(proj_dve.sem, 1)
                dve.wait_ge(*proj_dve.at(p, 6))
                v.tensor_reduce(bcq[:, :, 2, 0:T], prod[:, :, :].rearrange("p j (t n) -> p j t n", t=T),
                                AXIS.X, ALU.add).then_inc(proj_dve.sem, 1)
                src = bcq
                for s, rest in enumerate((res1, res2, None)):
                    dve.wait_ge(*proj_dve.at(p, 7 + 2 * s))
                    v.tensor_copy(split[:, :, :, s, :], src[:, :, :, :]).then_inc(proj_dve.sem, 1)
                    if rest is not None:
                        dve.wait_ge(*proj_dve.at(p, 8 + 2 * s))
                        v.tensor_tensor(rest[:, :, :, :], src[:, :, :, :], split[:, :, :, s, :], ALU.subtract) \
                            .then_inc(proj_dve.sem, 1)
                        src = rest

            def proj_2(p):
                dve.wait_ge(*softplus_act.at(p))
                v.tensor_scalar(rem[:, :], ex[:, :], 1.0, 1.0, ALU.add, ALU.subtract).then_inc(softplus_dve.sem, 1)
                v.scalar_tensor_tensor(sp_t[:, :], xd[:, :], 0.0, lnu[:, :], ALU.max, ALU.add) \
                    .then_inc(softplus_dve.sem, 1)
                dve.wait_ge(*softplus_dve.at(p, 1))
                v.tensor_tensor(rem[:, :], ex[:, :], rem[:, :], ALU.subtract).then_inc(softplus_dve.sem, 1)
                dve.wait_ge(*softplus_dve.at(p, 3))
                v.tensor_tensor(sp_t[:, :], sp_t[:, :], rem[:, :], ALU.add).then_inc(softplus_dve.sem, 1)

            def proj_3(p):
                dve.wait_ge(*rms_act.at(p))
                for m in range(4):
                    v.scalar_tensor_tensor(tile(dn[:, :], m), tile(sp_t[:, :], m), ms[:, 2, m:m + 1],
                                           rms_t[:, :].rearrange("p (k d) -> p k d", k=K3),
                                           ALU.mult, ALU.mult).then_inc(delta_dve.sem, 1)

            def bc_copy(p, par):
                dve.wait_ge(*bc_pe.at(p))
                for k, dst in enumerate((bT, cT, qT)):
                    v.tensor_copy(dst[:, par, 1:SEG].rearrange("p (j w) -> p j w", j=2),
                                  front_bf[0:96, k * 256:k * 256 + 200].rearrange("p (j w) -> p j w", j=2)[:, :, 0:HT]) \
                        .then_inc(bc_dve.sem, 1)

            def g_make(p):
                dve.wait_ge(*lnd_act.at(p, 2))
                v.tensor_tensor(gT[:, :, 1:], xnT[:, :, 1:], xnT[:, :, 0:SEQ], ALU.add).then_inc(g_dve.sem, 1)
                dve.wait_ge(*g_dve.at(p, 1))
                v.scalar_tensor_tensor(gT[:, :, 1:], sqT[:, :, :], 0.25, gT[:, :, 1:], ALU.mult, ALU.mult) \
                    .then_inc(g_dve.sem, 1)

            def dot_term(q, par):
                dve.wait_ge(*dot_pe.at(q))
                dve.wait_ge(*g_dve.at(q))
                v.tensor_tensor(acc[:, par, :].rearrange("p (k w) -> p k w", k=K3), gT[:, :, :],
                                b_ps[:, 0, 0:SEG].unsqueeze(1).broadcast_to([128, K3, SEG]), ALU.mult) \
                    .then_inc(acc_dve.sem, 1)

            def v_make(q, g):
                dve.wait_ge(*b_pe.at(q, g + 1))
                if not (first(q) and g < 2):
                    dve.wait_ge(*z_pool.at(q, g - 1))
                for_states = gT[:, :, :].unsqueeze(1).broadcast_to([128, 2, K3, SEG])
                for_blocks = b_ps[:, g % 2, 0:2 * SEG].rearrange("p (u w) -> p u w", u=2).unsqueeze(2) \
                    .broadcast_to([128, 2, K3, SEG])
                v.tensor_tensor(v_buf[:, g % 2, 1:].rearrange("p (u k w) -> p u k w", u=2, k=K3),
                                for_states, for_blocks, ALU.mult).then_inc(v_dve.sem, 1)

            def scan_group(q, g):
                dve.wait_ge(*z_pool.at(q, g + 1))
                dve.wait_ge(*a_act.at(q, 6 * g + 6))
                if not (first(q) and g < 2):
                    dve.wait_ge(*y_pool.at(q, 2 * (g - 1)))
                v.tensor_tensor_scan(p_buf[:, g % 2, :], z_buf[:, g % 2, :], a_ring[:, g, :], 0.0, ALU.add, ALU.mult) \
                    .then_inc(scan_dve.sem, 1)
                dve.wait_ge(*c_pe.at(q, g + 1))
                dve.wait_ge(*scan_dve.at(q, g + 1))
                s = p_buf[:, g % 2, :].rearrange("p (u k w) -> p u k w", u=2, k=K3)
                for_blocks = c_ps[:, g % 2, 0:2 * SEG].rearrange("p (u w) -> p u w", u=2).unsqueeze(2) \
                    .broadcast_to([128, 2, K3, SEG])
                v.tensor_tensor(s, s, for_blocks, ALU.mult) \
                    .then_inc(p_dve.sem, 1)

            def back_1(p, par):
                dve.wait_ge(*hres_ready.at(p))
                for j in range(2):
                    dve.wait_ge(*yT_pe.at(p, j + 1))
                    cols = slice(j * T * D, (j + 1) * T * D)
                    v.tensor_tensor(h2[:, cols], hres[:, par, cols], back_ps[0:HT, j, 0:T * D], ALU.add) \
                        .then_inc(h2_dve.sem, 1)
                dve.wait_ge(*h2_dve.at(p, 2))
                statistics(p, h2, bn6c, mv3, h2_dve, 2)

            def back_2(p):
                dve.wait_ge(*h2_rstd.at(p))
                if not first(p):
                    dve.wait_ge(*out_stored.at(p - 1))
                normalise(x2, h2, mv3, rs3, x2_dve)

            def back_3(p):
                s = route_dve
                dve.wait_ge(*logit_pe.at(p))
                v.tensor_tensor(lg[:, :, :].rearrange("p (t j) e -> p t j e", t=T),
                                back_ps[0:HT, :, 0:2 * E].rearrange("p t (j e) -> p t j e", j=2),
                                br_t[:, :].unsqueeze(1).unsqueeze(1).broadcast_to([HT, T, 2, E]), ALU.add).then_inc(s.sem, 1)
                dve.wait_ge(*s.at(p, 1))
                v.tensor_reduce(lmax[:, 0, :], lg[:, :, :], AXIS.X, ALU.max).then_inc(s.sem, 1)
                dve.wait_ge(*s.at(p, 2))
                v.tensor_tensor(lg[:, :, :], lg[:, :, :], lmax[:, 0, :].unsqueeze(2).broadcast_to([HT, 4, E]),
                                ALU.subtract).then_inc(s.sem, 1)
                dve.wait_ge(*s.at(p, 3))
                v.tensor_scalar(rank[:, :, :], lg[:, :, :], 0.0, None, ALU.is_equal).then_inc(s.sem, 1)
                dve.wait_ge(*s.at(p, 4))
                v.tensor_tensor(rank[:, :, :], rank[:, :, :], over_tiles(desc[:, :], E), ALU.mult).then_inc(s.sem, 1)
                dve.wait_ge(*s.at(p, 5))
                v.tensor_reduce(lmax[:, 1, :], rank[:, :, :], AXIS.X, ALU.max).then_inc(s.sem, 1)
                dve.wait_ge(*s.at(p, 6))
                v.tensor_tensor(oh[:, :, :], rank[:, :, :], lmax[:, 1, :].unsqueeze(2).broadcast_to([HT, 4, E]),
                                ALU.is_equal).then_inc(s.sem, 1)

            def back_4(p):
                dve.wait_ge(*onehot_pe.at(p))
                v.tensor_copy(ohT[:, :], back_ps[0:E, 1, 0:T * SEQ]).then_inc(onehot_dve.sem, 1)
                for t in range(T):
                    v.tensor_scalar(miss[t * DB:t * DB + E, :], back_ps[0:E, 1, t * SEQ:(t + 1) * SEQ], -1.0, None,
                                    ALU.add).then_inc(onehot_dve.sem, 1)

            def back_5(p):
                s = out_dve
                dve.wait_ge(*route_act.at(p))
                v.tensor_reduce(pm[:, 0, :], er[:, :, :], AXIS.X, ALU.add).then_inc(s.sem, 1)
                dve.wait_ge(*s.at(p, 1))
                v.reciprocal(pm[:, 1, :], pm[:, 0, :]).then_inc(s.sem, 1)
                dve.wait_ge(*s.at(p, 2))
                for m in range(4):
                    if m % 2 == 0:
                        dve.wait_ge(*ffn_pe.at(p, m // 2 + 1))
                    made = back_ps[0:HT, m // 2, (m % 2) * D:(m % 2 + 1) * D].rearrange("p (k d) -> p k d", k=K3)
                    v.scalar_tensor_tensor(tile(o_t[:, :], m), made, pm[:, 1, m:m + 1], tile(h2[:, :], m),
                                           ALU.mult, ALU.add).then_inc(s.sem, 1)

            def iteration(q, par):
                scan, front, tok, back, last = (alive(q + o) for o in (0, 1, 2, -1, -2))

                def step(g):
                    if scan and g + 1 < G:
                        v_make(q, g + 1)
                    if front and g + 1 == G:
                        v_make(q + 1, 0)
                    if scan:
                        scan_group(q, g)

                step(0)
                step(1)
                if front:
                    proj_1(q + 1)
                step(2)
                if last:
                    back_5(q - 2)
                if front:
                    proj_2(q + 1)
                if back:
                    back_1(q - 1, 1 - par)
                step(3)
                if front:
                    proj_3(q + 1)
                if back:
                    back_2(q - 1)
                if tok:
                    tok_1(q + 2)
                step(4)
                if front:
                    bc_copy(q + 1, 1 - par)
                if back:
                    back_3(q - 1)
                if tok:
                    tok_2(q + 2)
                if back:
                    back_4(q - 1)
                step(5)
                if tok:
                    tok_3(q + 2)
                step(6)
                if front:
                    g_make(q + 1)
                    dot_term(q + 1, 1 - par)
                step(7)

            for q in (-2, -1, 0, 1):
                iteration(q, q % 2)
            with dve.Fori(0, (PAIRS - 4) // 2) as i:
                iteration(i * 2 + 2, 0)
                iteration(i * 2 + 3, 1)
            for q in range(PAIRS - 2, PAIRS + 2):
                iteration(q, q % 2)


_INS = ["x", "cls_tok", "L0_tok_conv_w", "L0_tok_class_emb", "L0_tok_pos_emb", "L0_tok_M_diag", "L0_tok_M_a",
        "L0_tok_M_b", "L0_tok_ln_w", "L0_tok_ln_b", "L0_attn_A_log", "L0_attn_D_param", "L0_attn_W_bc",
        "L0_attn_W_dt", "L0_attn_W_dtp", "L0_attn_b_dt", "L0_attn_rms_scale", "L0_ffn_enc_w", "L0_ffn_enc_b",
        "L0_ffn_sw_w", "L0_ffn_sw_b", "L0_ffn_w1", "L0_ffn_b1", "L0_ffn_w2", "L0_ffn_b2"]


def shape_constants():
    import numpy as np

    ident = np.eye(128, dtype=np.float32)
    eye_split = np.ascontiguousarray(np.eye(D, dtype=np.float32).reshape(2, 96, D).transpose(1, 0, 2))
    one, mask_bits = (np.array([f], np.float32).view(np.uint16)[1] for f in (1.0, MASK))
    pick = np.zeros((3, T, N, N, 128), np.uint16)
    dot = np.zeros((3, T * N, 128), np.uint16)
    for t in range(T):
        for n in range(N):
            pick[:, t, n, n, t * DB:(t + 1) * DB] = one
        dot[:, t, t * DB:(t + 1) * DB] = one
    mask = np.repeat(np.eye(E, dtype=np.uint16) * mask_bits, ER, axis=1)
    desc = np.tile(np.arange(E, 0, -1, dtype=np.float32), (HT, 1))
    return {"ident": ident, "eye_split": eye_split, "state_pick": pick.reshape(3 * T * N, N, 128),
            "dot_pick": dot.reshape(3 * T * N, 128), "expert_mask": mask, "rank_desc": desc}


def kernel(**inputs):
    import numpy as _np
    import concourse.bacc as _bacc
    from concourse import mybir as _mybir
    from concourse.bass_utils import run_bass_kernel_spmd as _run

    nc = _bacc.Bacc("TRN2", target_bir_lowering=False, num_devices=1)
    arrays, args = {}, []
    for name, value in [(n, inputs[n]) for n in _INS] + list(shape_constants().items()):
        a = _np.ascontiguousarray(value)
        arrays[f"in_{name}_dram"] = a
        args.append(nc.dram_tensor(f"in_{name}_dram", a.shape, _mybir.dt.from_np(a.dtype), kind="ExternalInput").ap())
    args.append(nc.dram_tensor("out_0_dram", (B, SEQ, D), FP32, kind="ExternalOutput").ap())
    build_program(nc, *args)
    r = _run(nc, [arrays], core_ids=[0])
    return r.results[0]["out_0_dram"]
```

```python
import math

import concourse.bass as bass
from concourse import mybir
from contextlib import ExitStack

FP32 = mybir.dt.float32
BF16 = mybir.dt.bfloat16
ALU = mybir.AluOpType
ACT = mybir.ActivationFunctionType
AXIS = mybir.AxisListType

B, CH, IMG = 64, 3, 224
P, HP = 16, 14
D, N, R, NM = 192, 16, 48, 3
RANK, E, ER = 64, 8, 64
SEQ = HP * HP + 2
HT = SEQ // 2
PAIRS = B // 2
T = 2
DB = 64
K3 = D // DB
W = D + 2 * N
SEG = SEQ + 1
G = N // 2
BW = K3 * SEG
GW = 2 * BW
PH = P // 2
KR = CH * P
KP = 64 + KR
HC = E * ER // 128
MC = 2 * NM
LN_EPS = 1e-5
RMS_EPS = 1e-6
CLAMP_MID = (10.0 + 0.0001) / 2.0
CLAMP_HALF = (10.0 - 0.0001) / 2.0
MASK = float(2.0 ** 60)
ZEROS_LOADS = 5
ZEROS_FIRST = 12
ZEROS_ALL = ZEROS_FIRST + 2
FOLD_MIXED = 2 + MC
FOLD_CLASS = FOLD_MIXED + 1
FOLD_SPREAD = FOLD_CLASS + 14
FOLD_ALL = FOLD_SPREAD + 7


class Signal:

    def __init__(self, sem, steps):
        self.sem, self.steps = sem, steps

    def at(self, pair, k=None):
        return self.sem, pair * self.steps + (self.steps if k is None else k)


def first(pair):
    return isinstance(pair, int) and pair == 0


def alive(pair):
    return not isinstance(pair, int) or 0 <= pair < PAIRS


def build_program(nc, x, cls_tok, conv_w, class_emb, pos_emb, M_diag, M_a, M_b, ln_w, ln_b, A_log, D_param,
                  W_bc, W_dt, W_dtp, b_dt, rms_scale, enc_w, enc_b, sw_w, sw_b, w1, b1, w2, b2,
                  ident, eye_split, state_pick, dot_pick, expert_mask, rank_desc, out):
    ctx = ExitStack()
    with ctx:
        def sb(name, shape, dt=FP32):
            return ctx.enter_context(nc.sbuf_tensor(name, shape, dt))

        def pb(name, shape, dt=FP32):
            return ctx.enter_context(nc.psum_tensor(name, shape, dt))

        def signal(name, steps):
            return Signal(ctx.enter_context(nc.semaphore(name)), steps)

        idn = sb("idn", [128, 128])
        idb = sb("idb", [128, 128], BF16)
        eps = sb("eps", [128, 4])
        pick = sb("pick", [3 * T * N, N, 128], BF16)
        dpick = sb("dpick", [3 * T * N, 128], BF16)
        emask = sb("emask", [E, E * ER], BF16)
        desc = sb("desc", [HT, E])
        w_eff = sb("w_eff", [KP, PH, D])
        tok_bias = sb("tok_bias", [HT, 2, D])
        lnw = sb("lnw", [HT, 2, D])
        lnb = sb("lnb", [HT, 2, D])
        dpar = sb("dpar", [HT, 2, D])
        rms_t = sb("rms_t", [HT, D])
        a_bias = sb("a_bias", [128, K3, N])
        wp = sb("wp", [128, 2, W])
        w1_s = sb("w1_s", [128, 2, E * ER])
        wr = sb("wr", [128, 2, E])
        w2_s = sb("w2_s", [128, HC, D])
        b1_s = sb("b1_s", [128, HC])
        b2_s = sb("b2_s", [E, D])
        br_t = sb("br_t", [HT, E])
        x_img = sb("x_img", [KP, T, SEQ * P])
        bn6 = sb("bn6", [HT, 4, 6])
        mv1 = sb("mv1", [HT, 4, 2])
        mv2 = sb("mv2", [HT, 4, 2])
        mv3 = sb("mv3", [HT, 4, 2])
        six_count = sb("six_count", [HT, 4])
        bn6b = sb("bn6b", [HT, 4, 6])
        bn6c = sb("bn6c", [HT, 4, 6])
        neg_mean2 = sb("neg_mean2", [HT, 4])
        neg_mean3 = sb("neg_mean3", [HT, 4])
        shift2 = sb("shift2", [HT, 4])
        shift3 = sb("shift3", [HT, 4])
        rs1 = sb("rs1", [HT, 2, 4])
        rs2 = sb("rs2", [HT, 2, 4])
        rs3 = sb("rs3", [HT, 2, 4])
        h_tok = sb("h_tok", [HT, 4 * D])
        xn = sb("xn", [HT, 4 * D])
        hres = sb("hres", [HT, 2, 4 * D])
        xr = sb("xr", [HT, 4 * D])
        xrT = sb("xrT", [128, 2, T * SEQ])
        xnT = sb("xnT", [128, 3, SEG])
        xd = sb("xd", [HT, 4 * D])
        nx = sb("nx", [HT, 4 * D])
        ex = sb("ex", [HT, 4 * D])
        lnu = sb("lnu", [HT, 4 * D])
        rem = sb("rem", [HT, 4 * D])
        sp_t = xd
        ms = sb("ms", [HT, 3, 4])
        dn, lnd = ex, lnu
        bcq = sb("bcq", [HT, 2, 3, T * N])
        prod = sb("prod", [HT, 2, T * N])
        res1 = sb("res1", [HT, 2, 3, T * N])
        res2 = sb("res2", [HT, 2, 3, T * N])
        split = sb("split", [HT, 2, 3, 3, T * N], BF16)
        bT = sb("bT", [96, 2, SEG + 1], BF16)
        cT = sb("cT", [96, 2, SEG + 1], BF16)
        qT = sb("qT", [96, 2, SEG + 1], BF16)
        ldT = sb("ldT", [128, 3, SEQ])
        sqT = sb("sqT", [128, 3, SEQ])
        gT = sb("gT", [128, 3, SEG])
        v_buf = sb("v_buf", [128, 2, 1 + GW])
        z_buf = sb("z_buf", [128, 2, GW])
        a_ring = sb("a_ring", [128, G, GW])
        p_buf = sb("p_buf", [128, 2, GW])
        acc = sb("acc", [128, 2, BW])
        h2 = sb("h2", [HT, 4 * D])
        x2 = sb("x2", [HT, 4 * D])
        x2T = sb("x2T", [128, 2, T * SEQ])
        lg = sb("lg", [HT, 4, E])
        lmax = sb("lmax", [HT, 3, 4])
        oh = sb("oh", [HT, 4, E])
        rank = sb("rank", [HT, 4, E])
        er = sb("er", [HT, 4, E])
        pm = sb("pm", [HT, 2, 4])
        ohT = sb("ohT", [E, T * SEQ])
        miss = sb("miss", [E, T * SEQ], BF16)
        hid = sb("hid", [128, HC, T * SEQ])
        o_t = x2
        ring = a_ring[:, :, :].rearrange("p g w -> p (g w)")
        conv_s = ring[0:96, 0:MC * 768].rearrange("p (k n) -> p k n", k=MC)
        m_full = ring[0:96, 4608:4608 + MC * D].rearrange("p (k n) -> p k n", k=MC)
        ma_s = ring[0:96, 5760:5760 + MC * RANK].rearrange("p (k n) -> p k n", k=MC)
        maT = ring[0:RANK, 6144:6144 + MC * 96].rearrange("p (k n) -> p k n", k=MC)
        mb_s = ring[0:RANK, 6720:6720 + D]
        md_s = ring[0:96, 6912:6912 + MC]
        eyes = ring[0:96, 6920:6920 + 2 * D].rearrange("p (k n) -> p k n", k=2)
        wdt_s = ring[:, 7304:7304 + 2 * R].rearrange("p (k n) -> p k n", k=2)
        wdtT = ring[0:R, 7400:7400 + D]
        wdtp_s = ring[0:R, 7592:7592 + D]
        enc_s = ring[:, 7784:7784 + 2 * ER].rearrange("p (k n) -> p k n", k=2)
        encT = ring[0:ER, 7912:7912 + D]
        sw_s = ring[0:ER, 8104:8104 + E]
        encb_s = ring[0:ER, 8112:8113]
        encb_r = ring[0:ER, 8120:8120 + HT]
        swb_s = ring[0:HT, 8220:8220 + E]
        alog_s = ring[:, 8228:8228 + K3 * N].rearrange("p (k n) -> p k n", k=K3)
        vflat = v_buf[:, :, :].rearrange("p k w -> p (k w)")
        pos_s = vflat[0:HT, 0:2 * NM * D].rearrange("p (j n) -> p j n", j=2)
        cls_s = z_buf[0:HT, :, :].rearrange("p k w -> p (k w)")[:, 0:NM * D]
        posT = p_buf[0:96, :, :].rearrange("p k w -> p (k w)")[:, 0:2 * MC * HT].rearrange(
            "p (j k t) -> p j k t", j=2, k=MC)

        b_ps = pb("b_ps", [128, 2, 512])
        c_ps = pb("c_ps", [128, 2, 512])
        front_ps = pb("front_ps", [128, 2, 512])
        back_ps = pb("back_ps", [128, 2, 512])
        fold_banks = (front_ps[:, 0, :], front_ps[:, 1, :], c_ps[:, 0, :], c_ps[:, 1, :])
        front_bf = front_ps[:, 0, :].bitcast(BF16)

        def tile(t, m):
            return t.rearrange("p (j k t d) -> p j t k d", j=2, k=K3, t=T)[:, m % 2, m // 2]

        def rows_of(t, m):
            return t[:, m * D:(m + 1) * D]

        def by_image(t):
            return t.rearrange("p (a t d) -> p t a d", a=2 * K3, t=T)

        def over_images(t):
            return t.rearrange("p j (k d) -> p (j k) d", k=K3).unsqueeze(1).broadcast_to([HT, T, 2 * K3, DB])

        mixing_in = signal("mixing_in", 0)
        weights_in = signal("weights_in", 0)
        zeros_set = signal("zeros_set", 0)
        fold_pe = signal("fold_pe", 0)
        fold_dve = signal("fold_dve", 0)
        consts_set = signal("consts_set", 0)
        x_in = [signal(f"x_in{t}", 2 * CH * 16) for t in range(T)]
        out_stored = signal("out_stored", T * 16)
        tokens_pe = signal("tokens_pe", 4)
        tok_stats = signal("tok_stats", 13)
        tok_rstd = signal("tok_rstd", 2)
        h_ready = signal("h_ready", 14)
        h_rstd = signal("h_rstd", 2)
        xn_ready = signal("xn_ready", 4)
        hres_ready = signal("hres_ready", 2)
        xr_ready = signal("xr_ready", 8)
        xrT_pe = signal("xrT_pe", 2)
        xrT_act = signal("xrT_act", 2)
        xnT_pe = signal("xnT_pe", 2)
        xnT_act = signal("xnT_act", 2)
        proj_pe = signal("proj_pe", 4)
        bc_act = signal("bc_act", 2)
        proj_dve = signal("proj_dve", 7)
        softplus_act = signal("softplus_act", 10)
        softplus_pool = signal("softplus_pool", 1)
        softplus_dve = signal("softplus_dve", 3)
        rms_act = signal("rms_act", 6)
        delta_dve = signal("delta_dve", 4)
        clamp_act = signal("clamp_act", 2)
        bc_pe = signal("bc_pe", 1)
        bc_dve = signal("bc_dve", 3)
        lnd_pe = signal("lnd_pe", 2)
        lnd_act = signal("lnd_act", 4)
        g_dve = signal("g_dve", 2)
        dot_pe = signal("dot_pe", 1)
        acc_dve = signal("acc_dve", 1)
        b_pe = signal("b_pe", G)
        c_pe = signal("c_pe", G)
        v_dve = signal("v_dve", G)
        z_pool = signal("z_pool", G)
        a_act = signal("a_act", 6 * G)
        scan_dve = signal("scan_dve", G)
        p_dve = signal("p_dve", G)
        y_pool = signal("y_pool", 2 * G)
        yT_pe = signal("yT_pe", 2)
        h2_dve = signal("h2_dve", 12)
        h2_rstd = signal("h2_rstd", 2)
        x2_act = signal("x2_act", 8)
        x2T_pe = signal("x2T_pe", 2)
        x2T_act = signal("x2T_act", 2)
        logit_pe = signal("logit_pe", 1)
        route_dve = signal("route_dve", 7)
        route_act = signal("route_act", 1)
        onehot_pe = signal("onehot_pe", 1)
        onehot_dve = signal("onehot_dve", 2)
        hid_pe = signal("hid_pe", HC)
        hid_act = signal("hid_act", HC)
        ffn_pe = signal("ffn_pe", 2)
        out_dve = signal("out_dve", 6)

        block = ctx.enter_context(nc.Block())
        x_v = x.rearrange("b c (h p) w -> b c p h w", p=P)
        out_v = out.rearrange("(q t) (j p) d -> q t p j d", t=T, j=2)
        MIXING_LOADS, SETUP_LOADS = [], []

        @block.sync
        def _(sp):
            mixing, weights = [0], [0]

            def load(dst, src, columns=False, done=weights_in, n=weights):
                sp.dma_start(dst, src, allow_slow_non_contiguous=columns).then_inc(done.sem, 16)
                n[0] += 1

            def load_x(p, t):
                if not first(p):
                    sp.wait_ge(*tokens_pe.at(p - 1, 2 * t + 2))
                for half in range(2):
                    for c in range(CH):
                        row = 64 * half + P * c
                        dst = x_img[row:row + P, t, 2 * P:].rearrange("p (h w) -> p h w", h=HP)
                        sp.dma_start(dst[:, :, 0:IMG - PH * half], x_v[p * T + t, c, :, :, PH * half:]) \
                          .then_inc(x_in[t].sem, 16)

            def store(p):
                sp.wait_ge(*out_dve.at(p))
                for t in range(T):
                    sp.dma_start(out_v[p, t], o_t[:, 2 * t * D:2 * (t + 1) * D].rearrange("p (j d) -> p j d", j=2)) \
                      .then_inc(out_stored.sem, 16)

            first_loads = dict(done=mixing_in, n=mixing)
            load(idn[:, :], ident, **first_loads)
            load(ma_s, M_a.rearrange("(k p) r -> p k r", p=96), **first_loads)
            load(mb_s, M_b, **first_loads)
            load(md_s, M_diag.rearrange("(k p) -> p k", p=96), columns=True, **first_loads)
            load(eyes, eye_split, **first_loads)
            load(conv_s, conv_w.rearrange("m (k p) n -> p (m k) n", p=96), **first_loads)
            MIXING_LOADS.append(16 * mixing[0])
            sp.wait_ge(zeros_set.sem, ZEROS_LOADS)
            for t in range(T):
                load_x(0, t)
            load(pos_s[1:HT, 0, :].rearrange("p (m e) -> p m e", m=NM), pos_emb[:, 0:HT - 1, :].rearrange("m s e -> s m e"))
            load(pos_s[:, 1, :].rearrange("p (m e) -> p m e", m=NM), pos_emb[:, HT - 1:, :].rearrange("m s e -> s m e"))
            load(cls_s[1:2, :].rearrange("p (m e) -> p m e", m=NM), class_emb.rearrange("(o m) e -> o m e", o=1))
            load(wdt_s[:, 0, :], W_dt[0:128, :])
            load(wdt_s[0:DB, 1, :], W_dt[128:D, :])
            load(wdtp_s, W_dtp)
            load(enc_s[:, 0, :], enc_w[0:128, :])
            load(enc_s[0:DB, 1, :], enc_w[128:D, :])
            load(sw_s, sw_w)
            load(encb_s, enc_b.rearrange("(p o) -> p o", o=1), columns=True)
            load(swb_s, sw_b.partition_broadcast(HT))
            for t in range(T):
                rows = slice(t * DB, (t + 1) * DB)
                load(alog_s[rows, :, :], A_log.rearrange("(k p) n -> p k n", k=K3))
            load(w1_s[:, 0, :].rearrange("d (e r) -> d e r", e=E), w1[:, 0:128, :].rearrange("e d r -> d e r"))
            load(w1_s[0:DB, 1, :].rearrange("d (e r) -> d e r", e=E), w1[:, 128:D, :].rearrange("e d r -> d e r"))
            for j in range(2):
                load(lnw[j == 0:HT, j, :], ln_w.partition_broadcast(HT - (j == 0)))
                load(lnb[j == 0:HT, j, :], ln_b.partition_broadcast(HT - (j == 0)))
                load(dpar[:, j, :], D_param.partition_broadcast(HT))
            load(lnb[0:1, 0, :], cls_tok[0, :, :])
            load(wp[:, 0, D:W], W_bc[0:128, :])
            load(wp[0:DB, 1, D:W], W_bc[128:D, :])
            load(wp[DB:DB + 1, 1, 0:D], b_dt.rearrange("(o d) -> o d", o=1))
            load(rms_t[:, :], rms_scale.partition_broadcast(HT))
            load(w2_s[:, :, :], w2.rearrange("(c e) r d -> (e r) c d", e=2))
            load(b1_s[:, :], b1.rearrange("(c e) r -> (e r) c", e=2), columns=True)
            load(b2_s[:, :], b2)
            load(pick[:, :, :], state_pick.bitcast(BF16))
            load(dpick[:, :], dot_pick.bitcast(BF16))
            load(emask[:, :], expert_mask.bitcast(BF16))
            load(desc[:, :], rank_desc)
            SETUP_LOADS.append(16 * weights[0])

            def iteration(q):
                if alive(q - 2):
                    store(q - 2)
                for t in range(T):
                    if alive(q + 3):
                        load_x(q + 3, t)

            for q in (-2, -1, 0, 1):
                iteration(q)
            with sp.Fori(0, PAIRS - 5) as i:
                iteration(i + 2)
            for q in range(PAIRS - 3, PAIRS + 2):
                iteration(q)
            sp.wait_ge(*out_stored.at(PAIRS - 1))

        @block.gpsimd
        def _(pool):
            for view in (pos_s[0:1, 0, :], cls_s, lnw[0:1, 0, :], lnb[0:1, 0, :], x_img[:, :, :], w_eff[:, :, :],
                         xnT[:, :, 0:1], gT[:, :, 0:1], bT[:, :, :], cT[:, :, :], qT[:, :, :],
                         bcq[:, :, :, :]):
                nc.gpsimd.memset(view, 0.0).then_inc(zeros_set.sem, 1)
            pool.wait_ge(fold_dve.sem, FOLD_ALL)
            nc.gpsimd.memset(a_ring[:, :, :].rearrange("p g (k w) -> p (g k) w", w=SEG)[:, :, 0:1], 0.0) \
                .then_inc(zeros_set.sem, 1)
            nc.gpsimd.memset(v_buf[:, :, 0:1], 0.0).then_inc(zeros_set.sem, 1)

            def z_sum(q, g):
                pool.wait_ge(*v_dve.at(q, g + 1))
                if not (first(q) and g < 2):
                    pool.wait_ge(*scan_dve.at(q, g - 1))
                nc.gpsimd.tensor_tensor(z_buf[:, g % 2, :], v_buf[:, g % 2, 1:1 + GW], v_buf[:, g % 2, 0:GW], ALU.add) \
                    .then_inc(z_pool.sem, 1)

            def state_sum(q, g, par):
                pool.wait_ge(*p_dve.at(q, g + 1))
                if g == 0:
                    pool.wait_ge(*acc_dve.at(q))
                for u in range(2):
                    if not (first(q) and g == 0 and u == 0):
                        pool.wait_ge(*y_pool.at(q, 2 * g + u))
                    nc.gpsimd.tensor_tensor(acc[:, par, :], acc[:, par, :], p_buf[:, g % 2, u * BW:(u + 1) * BW],
                                            ALU.add).then_inc(y_pool.sem, 1)

            def softplus_rest(p):
                pool.wait_ge(*softplus_dve.at(p, 1))
                nc.gpsimd.tensor_tensor(rem[:, :], ex[:, :], rem[:, :], ALU.subtract).then_inc(softplus_pool.sem, 1)

            def residual(p, par):
                pool.wait_ge(*xn_ready.at(p))
                if not (isinstance(p, int) and p < 2):
                    pool.wait_ge(*h2_dve.at(p - 2, 2))
                nc.gpsimd.tensor_tensor(by_image(hres[:, par, :]), by_image(xn[:, :]), over_images(dpar[:, :, :]),
                                        ALU.mult).then_inc(hres_ready.sem, 1)
                pool.wait_ge(*hres_ready.at(p, 1))
                nc.gpsimd.tensor_tensor(hres[:, par, :], hres[:, par, :], h_tok[:, :], ALU.add) \
                    .then_inc(hres_ready.sem, 1)

            def iteration(q, par):
                front, scan = (alive(q + o) for o in (1, 0))
                if scan:
                    state_sum(q, 1, par)
                if front:
                    softplus_rest(q + 1)
                if scan:
                    z_sum(q, 3)
                    state_sum(q, 2, par)
                    z_sum(q, 4)
                if front:
                    residual(q + 1, 1 - par)
                if scan:
                    state_sum(q, 3, par)
                    z_sum(q, 5)
                    state_sum(q, 4, par)
                    z_sum(q, 6)
                    state_sum(q, 5, par)
                    z_sum(q, 7)
                    state_sum(q, 6, par)
                if front:
                    z_sum(q + 1, 0)
                    z_sum(q + 1, 1)
                if scan:
                    state_sum(q, 7, par)
                if front:
                    state_sum(q + 1, 0, 1 - par)
                    z_sum(q + 1, 2)

            for q in (-1, 0, 1):
                iteration(q, q % 2)
            with pool.Fori(0, (PAIRS - 4) // 2) as i:
                iteration(i * 2 + 2, 0)
                iteration(i * 2 + 3, 1)
            for q in range(PAIRS - 2, PAIRS):
                iteration(q, q % 2)

        @block.scalar
        def _(act):
            act.wait_ge(fold_dve.sem, FOLD_ALL)

            def act_ln_exp():
                nc.scalar.preload_act_table_set("natural_log_exp_and_others")

            def act_tanh_gelu():
                nc.scalar.preload_act_table_set("gelu_and_others")

            def rstd(p, stats, mv, rs, done, k=None):
                act.wait_ge(*stats.at(p, k))
                nc.scalar.activation(rs[:, 0, :], mv[:, :, 1], ACT.Ln, bias=eps[0:HT, 0:1]).then_inc(done.sem, 1)
                act.wait_ge(*done.at(p, 1))
                nc.scalar.activation(rs[:, 1, :], rs[:, 0, :], ACT.Exp, scale=-0.5).then_inc(done.sem, 1)

            def xnT_copy(p):
                if not first(p):
                    act.wait_ge(*g_dve.at(p - 1))
                act.wait_ge(*xnT_pe.at(p))
                nc.scalar.activation(xnT[:, 0:2, 1:], front_ps[:, 0, 0:2 * SEQ].rearrange("p (k w) -> p k w", k=2),
                                     ACT.Copy).then_inc(xnT_act.sem, 1)
                nc.scalar.activation(xnT[:, 2, 1:], front_ps[:, 1, 0:SEQ], ACT.Copy).then_inc(xnT_act.sem, 1)

            def proj_copy(p):
                act.wait_ge(*proj_pe.at(p))
                if not first(p):
                    act.wait_ge(*clamp_act.at(p - 1))
                    act.wait_ge(*delta_dve.at(p - 1))
                    act.wait_ge(*proj_dve.at(p - 1))
                for k in range(2):
                    nc.scalar.activation(bcq[:, :, k, :].rearrange("p j (t n) -> p t j n", t=T),
                                         front_ps[0:HT, :, 0:2 * W].rearrange("p t (j w) -> p t j w", j=2)
                                         [:, :, :, D + N * k:D + N * (k + 1)], ACT.Copy).then_inc(bc_act.sem, 1)
                for dst, func in ((nx, ACT.Abs), (xd, ACT.Relu)):
                    for m in range(4):
                        nc.scalar.activation(tile(dst[:, :], m), front_ps[0:HT, m // 2, (m % 2) * W:(m % 2) * W + D]
                                             .rearrange("p (k d) -> p k d", k=K3), func).then_inc(softplus_act.sem, 1)

            def softplus(p):
                act.wait_ge(*softplus_act.at(p, 4))
                nc.scalar.activation(ex[:, :], nx[:, :], ACT.Exp, scale=-1.0).then_inc(softplus_act.sem, 1)
                act.wait_ge(*softplus_act.at(p, 9))
                nc.scalar.activation(lnu[:, :], ex[:, :], ACT.Ln, bias=1.0).then_inc(softplus_act.sem, 1)

            def rms(p):
                act.wait_ge(*softplus_dve.at(p))
                for m in range(4):
                    nc.scalar.activation(tile(rem[:, :], m), tile(sp_t[:, :], m), ACT.Square, accum_out=ms[:, 0, m:m + 1]) \
                        .then_inc(rms_act.sem, 1)
                act.wait_ge(*rms_act.at(p, 4))
                nc.scalar.activation(ms[:, 1, :], ms[:, 0, :], ACT.Ln, scale=1.0 / D, bias=eps[0:HT, 1:2]) \
                    .then_inc(rms_act.sem, 1)
                act.wait_ge(*rms_act.at(p, 5))
                nc.scalar.activation(ms[:, 2, :], ms[:, 1, :], ACT.Exp, scale=-0.5).then_inc(rms_act.sem, 1)

            def clamp_tanh(p):
                act.wait_ge(*delta_dve.at(p))
                nc.scalar.activation(nx[:, :], dn[:, :], ACT.Tanh, scale=1.0 / CLAMP_HALF, bias=eps[0:HT, 2:3]) \
                    .then_inc(clamp_act.sem, 1)

            def clamp_ln(p):
                act.wait_ge(*clamp_act.at(p, 1))
                nc.scalar.activation(lnd[:, :], nx[:, :], ACT.Ln, scale=CLAMP_HALF, bias=eps[0:HT, 3:4]) \
                    .then_inc(clamp_act.sem, 1)

            def lnd_copy(p):
                act.wait_ge(*lnd_pe.at(p))
                if not first(p):
                    act.wait_ge(*a_act.at(p - 1))
                ab = front_ps[:, 0, 0:2 * SEQ].rearrange("p (k w) -> p k w", k=2)
                tail = front_ps[:, 1, 0:SEQ]
                nc.scalar.activation(sqT[:, 0:2, :], ab, ACT.Exp, scale=0.5).then_inc(lnd_act.sem, 1)
                nc.scalar.activation(sqT[:, 2, :], tail, ACT.Exp, scale=0.5).then_inc(lnd_act.sem, 1)
                nc.scalar.activation(ldT[:, 0:2, :], ab, ACT.Copy).then_inc(lnd_act.sem, 1)
                nc.scalar.activation(ldT[:, 2, :], tail, ACT.Copy).then_inc(lnd_act.sem, 1)

            def decays(p, g):
                if g == 0:
                    act.wait_ge(*lnd_act.at(p))
                if not first(p):
                    act.wait_ge(*scan_dve.at(p - 1, g + 1))
                for u in range(2):
                    for k in range(K3):
                        col = (u * K3 + k) * SEG
                        nc.scalar.activation(a_ring[:, g, col + 1:col + SEG], ldT[:, k, :], ACT.Tanh, scale=-0.5,
                                             bias=a_bias[:, k, 2 * g + u:2 * g + u + 1]).then_inc(a_act.sem, 1)

            def normalise(p, dst, src, rs, neg_mean, shift, done, free):
                for m in range(4):
                    nc.scalar.activation(shift[:, m:m + 1], rs[:, 1, m:m + 1], ACT.Copy, scale=neg_mean[:, m:m + 1]) \
                        .then_inc(done.sem, 1)
                if not first(p):
                    for used in free:
                        act.wait_ge(*used.at(p - 1))
                for m in range(4):
                    act.wait_ge(*done.at(p, m + 1))
                    nc.scalar.activation(dst[m], tile(src[:, :], m), ACT.Identity, scale=rs[:, 1, m:m + 1],
                                         bias=shift[:, m:m + 1]).then_inc(done.sem, 1)

            def xn_normalise(p):
                rstd(p, h_ready, mv2, rs2, h_rstd)
                act.wait_ge(*h_rstd.at(p))
                normalise(p, [rows_of(xr, m).rearrange("p (k d) -> p k d", k=K3) for m in range(4)], h_tok, rs2, neg_mean2,
                          shift2, xr_ready, (xrT_pe,))

            def xn_pairs(p):
                if not first(p):
                    act.wait_ge(*xnT_pe.at(p - 1))
                    act.wait_ge(*hres_ready.at(p - 1))
                act.wait_ge(*xr_ready.at(p, 4))
                for m in range(4):
                    nc.scalar.activation(tile(xn[:, :], m), tile(h_tok[:, :], m), ACT.Identity, scale=rs2[:, 1, m:m + 1],
                                         bias=shift2[:, m:m + 1]).then_inc(xn_ready.sem, 1)

            def xrT_copy(p):
                act.wait_ge(*xrT_pe.at(p))
                nc.scalar.activation(xrT[:, 0, :], front_ps[:, 0, 0:T * SEQ], ACT.Copy).then_inc(xrT_act.sem, 1)
                nc.scalar.activation(xrT[0:DB, 1, :], front_ps[0:DB, 1, 0:T * SEQ], ACT.Copy).then_inc(xrT_act.sem, 1)

            def x2_normalise(p):
                rstd(p, h2_dve, mv3, rs3, h2_rstd)
                act.wait_ge(*h2_rstd.at(p))
                normalise(p, [rows_of(x2, m).rearrange("p (k d) -> p k d", k=K3) for m in range(4)], h2, rs3, neg_mean3,
                          shift3, x2_act, (out_stored,))

            def x2T_copy(p):
                act.wait_ge(*x2T_pe.at(p))
                nc.scalar.activation(x2T[:, 0, :], back_ps[:, 0, 0:T * SEQ], ACT.Copy).then_inc(x2T_act.sem, 1)
                nc.scalar.activation(x2T[0:DB, 1, :], back_ps[0:DB, 1, 0:T * SEQ], ACT.Copy).then_inc(x2T_act.sem, 1)

            def route_exp(p):
                act.wait_ge(*route_dve.at(p))
                nc.scalar.activation(er[:, :, :], lg[:, :, :], ACT.Exp).then_inc(route_act.sem, 1)

            def hidden(p, c):
                act.wait_ge(*hid_pe.at(p, c + 1))
                nc.scalar.activation(hid[:, c, :], back_ps[:, c % 2, 0:T * SEQ], ACT.Gelu, bias=b1_s[:, c:c + 1]) \
                    .then_inc(hid_act.sem, 1)

            def iteration(q):
                tok, front, scan, back = (alive(q + o) for o in (2, 1, 0, -1))
                act_tanh_gelu()
                if front:
                    clamp_tanh(q + 1)
                if back:
                    x2T_copy(q - 1)
                act_ln_exp()
                if tok:
                    rstd(q + 2, tok_stats, mv1, rs1, tok_rstd, 9)
                if front:
                    clamp_ln(q + 1)
                    lnd_copy(q + 1)
                if tok:
                    xn_normalise(q + 2)
                if back:
                    route_exp(q - 1)
                act_tanh_gelu()
                if front:
                    decays(q + 1, 0)
                if tok:
                    xn_pairs(q + 2)
                if front:
                    xnT_copy(q + 1)
                    decays(q + 1, 1)
                if tok:
                    xrT_copy(q + 2)
                if back:
                    hidden(q - 1, 0)
                if front:
                    decays(q + 1, 2)
                    decays(q + 1, 3)
                if back:
                    hidden(q - 1, 1)
                if front:
                    decays(q + 1, 4)
                    decays(q + 1, 5)
                if back:
                    hidden(q - 1, 2)
                if tok:
                    proj_copy(q + 2)
                if front:
                    decays(q + 1, 6)
                    decays(q + 1, 7)
                if back:
                    hidden(q - 1, 3)
                act_ln_exp()
                if tok:
                    softplus(q + 2)
                    rms(q + 2)
                if scan:
                    x2_normalise(q)

            for q in (-2, -1, 0, 1):
                iteration(q)
            with act.Fori(0, (PAIRS - 4) // 2) as i:
                iteration(i * 2 + 2)
                iteration(i * 2 + 3)
            for q in range(PAIRS - 2, PAIRS + 2):
                iteration(q)

        @block.tensor
        def _(pe):
            pe.wait_ge(mixing_in.sem, MIXING_LOADS[0])
            for k in range(MC):
                last = nc.tensor.transpose(front_ps[0:RANK, k // 4, (k % 4) * 96:(k % 4 + 1) * 96], ma_s[:, k, :],
                                           idn[0:96, 0:96])
            last.then_inc(fold_pe.sem, 1)
            pe.wait_ge(fold_dve.sem, 2)
            for k in range(MC):
                bank = back_ps[:, k // 2, :] if k < 4 else b_ps[:, 0, :]
                last = nc.tensor.matmul(bank[0:96, (k % 2) * D:(k % 2 + 1) * D], maT[:, k, :], mb_s,
                                        start=True, stop=True)
            last.then_inc(fold_pe.sem, 1)
            pe.wait_ge(fold_dve.sem, FOLD_MIXED)
            pixels = conv_s.rearrange("p k (r x) -> p k x r", x=P)
            for px in range(P):
                half, col = px // PH, px % PH
                for k in range(MC):
                    last = nc.tensor.matmul(fold_banks[col // 2][64 * half:64 * half + KR, (col % 2) * D:(col % 2 + 1) * D],
                                            pixels[:, k, px, :], m_full[:, k, :], start=k == 0, stop=k == MC - 1)
            pe.wait_ge(weights_in.sem, SETUP_LOADS[0])
            pe.wait_ge(fold_dve.sem, FOLD_CLASS)
            for jk in range(2 * MC):
                bank = (back_ps[:, 0, :], back_ps[:, 1, :], b_ps[:, 0, :])[jk // 4]
                last = nc.tensor.transpose(bank[0:96, (jk % 4) * HT:(jk % 4 + 1) * HT],
                                           pos_s[:, jk // MC, (jk % MC) * 96:(jk % MC + 1) * 96], idn[0:HT, 0:HT])
            for c, (w, cols) in enumerate(((wdt_s, R), (enc_s, ER))):
                nc.tensor.transpose(b_ps[0:cols, 1, c * D:c * D + 128], w[:, 0, :], idn[:, :])
                last = nc.tensor.transpose(b_ps[0:cols, 1, c * D + 128:(c + 1) * D], w[0:DB, 1, :], idn[0:DB, 0:DB])
            last.then_inc(fold_pe.sem, 1)
            pe.wait_ge(fold_dve.sem, FOLD_SPREAD)
            for j in range(2):
                for k in range(MC):
                    nc.tensor.matmul(back_ps[0:HT, 0, j * D:(j + 1) * D], posT[:, j, k, :], m_full[:, k, :],
                                     start=k == 0, stop=k == MC - 1)
            nc.tensor.matmul(front_ps[:, 0, 0:D], wdtT[:, 0:128], wdtp_s, start=True, stop=True)
            nc.tensor.matmul(front_ps[0:DB, 0, D:2 * D], wdtT[:, 128:D], wdtp_s, start=True, stop=True)
            nc.tensor.matmul(back_ps[:, 1, 0:E], encT[:, 0:128], sw_s, start=True, stop=True)
            nc.tensor.matmul(back_ps[0:DB, 1, E:2 * E], encT[:, 128:D], sw_s, start=True, stop=True)
            nc.tensor.matmul(b_ps[0:HT, 0, 0:E], encb_r, sw_s, start=True, stop=True).then_inc(fold_pe.sem, 1)
            pe.wait_ge(fold_dve.sem, FOLD_ALL)

            def tokens(p, m):
                t, j = m // 2, m % 2
                if j == 0:
                    pe.wait_ge(*x_in[t].at(p))
                if m == 0 and not first(p):
                    pe.wait_ge(*softplus_act.at(p - 1, 8))
                for px in range(PH):
                    pixels = x_img[:, t, j * HT * P:(j + 1) * HT * P].rearrange("p (s x) -> p x s", x=P)
                    nc.tensor.matmul(front_ps[0:HT, t, j * D:(j + 1) * D], pixels[:, px, :], w_eff[:, px, :],
                                            start=px == 0, stop=False)
                nc.tensor.matmul(front_ps[0:HT, t, j * D:(j + 1) * D], idn[0:HT, 0:HT], tok_bias[:, j, :],
                                 start=False, stop=True).then_inc(tokens_pe.sem, 1)

            def to_channels(src, dst, done):
                for k in range(K3):
                    for j in range(2):
                        col = j * T * D + k * 128
                        last = nc.tensor.transpose(dst[:, k // 2, (k % 2) * SEQ + j * HT:(k % 2) * SEQ + (j + 1) * HT],
                                                   src[:, col:col + 128], idn[0:HT, 0:HT])
                    if k:
                        last.then_inc(done.sem, 1)

            def rows_transpose(src, dst, done):
                for k, rows in enumerate((128, DB)):
                    for m in range(4):
                        last = nc.tensor.transpose(dst[0:rows, k, m * HT:(m + 1) * HT],
                                                   src[:, m * D + 128 * k:m * D + 128 * k + rows], idn[0:HT, 0:HT])
                    last.then_inc(done.sem, 1)

            def xr_transpose(p):
                pe.wait_ge(*xr_ready.at(p))
                if not first(p):
                    pe.wait_ge(*xnT_act.at(p - 1))
                rows_transpose(xr, front_ps, xrT_pe)

            def xn_transpose(p):
                pe.wait_ge(*xn_ready.at(p))
                pe.wait_ge(*lnd_act.at(p))
                to_channels(xn, front_ps, xnT_pe)

            def project(p, m):
                if m == 0:
                    pe.wait_ge(*xrT_act.at(p))
                t, j, cols = m // 2, m % 2, slice(m * HT, (m + 1) * HT)
                o = front_ps[0:HT, t, j * W:(j + 1) * W]
                nc.tensor.matmul(o, xrT[:, 0, cols], wp[:, 0, :], start=True, stop=False)
                nc.tensor.matmul(o, xrT[0:DB + 1, 1, cols], wp[0:DB + 1, 1, :], start=False, stop=True) \
                    .then_inc(proj_pe.sem, 1)

            def bc_transpose(p):
                pe.wait_ge(*proj_dve.at(p))
                if alive(p + 1):
                    pe.wait_ge(*tok_stats.at(p + 1))
                for j in range(2):
                    for k in range(3):
                        last = nc.tensor.transpose(front_bf[0:96, k * 256 + j * 100:k * 256 + j * 100 + HT],
                                                   split[:, j, k, :, :].rearrange("p s n -> p (s n)"), idb[0:HT, 0:HT])
                last.then_inc(bc_pe.sem, 1)

            def lnd_transpose(p):
                pe.wait_ge(*clamp_act.at(p))
                pe.wait_ge(*bc_dve.at(p))
                to_channels(lnd, front_ps, lnd_pe)

            def dot_fill(q, par):
                pe.wait_ge(*bc_dve.at(q))
                if not first(q):
                    pe.wait_ge(*v_dve.at(q - 1, G - 1))
                nc.tensor.matmul(b_ps[:, 0, 0:SEG], dpick[:, :], qT[:, par, 0:SEG], start=True, stop=True) \
                    .then_inc(dot_pe.sem, 1)

            def group_fill(bank, rows, g, par):
                for u in range(2):
                    last = nc.tensor.matmul(bank[:, u * SEG:(u + 1) * SEG], pick[:, 2 * g + u, :], rows[:, par, 0:SEG],
                                            start=True, stop=True)
                return last

            def b_fill(q, g, par):
                if g == 0:
                    pe.wait_ge(*acc_dve.at(q))
                elif not (first(q) and g < 2):
                    pe.wait_ge(*v_dve.at(q, g - 1))
                group_fill(b_ps[:, g % 2, :], bT, g, par).then_inc(b_pe.sem, 1)

            def c_fill(q, g, par):
                if not (first(q) and g < 2):
                    pe.wait_ge(*p_dve.at(q, g - 1))
                group_fill(c_ps[:, g % 2, :], cT, g, par).then_inc(c_pe.sem, 1)

            def y_transpose(p, par):
                pe.wait_ge(*y_pool.at(p))
                if not first(p):
                    pe.wait_ge(*out_dve.at(p - 1))
                for j in range(2):
                    for k in range(K3):
                        last = nc.tensor.transpose(back_ps[0:HT, j, k * 128:(k + 1) * 128],
                                                   acc[:, par, k * SEG + 1 + j * HT:k * SEG + 1 + (j + 1) * HT], idn[:, :])
                    last.then_inc(yT_pe.sem, 1)

            def x2_transpose(p):
                pe.wait_ge(*x2_act.at(p))
                rows_transpose(x2, back_ps, x2T_pe)

            def by_channels(o, columns, weights, last):
                nc.tensor.matmul(o, columns(0, 128), weights(0, 128), start=True, stop=False)
                return nc.tensor.matmul(o, columns(1, DB), weights(1, DB), start=False, stop=last)

            def logits(p):
                pe.wait_ge(*x2T_act.at(p))
                for m in range(4):
                    done = by_channels(back_ps[0:HT, m // 2, (m % 2) * E:(m % 2 + 1) * E],
                                       lambda k, rows: x2T[0:rows, k, m * HT:(m + 1) * HT],
                                       lambda k, rows: wr[0:rows, k, :], True)
                done.then_inc(logit_pe.sem, 1)

            def onehot_transpose(p):
                pe.wait_ge(*route_dve.at(p))
                for m in range(4):
                    last = nc.tensor.transpose(back_ps[0:E, 1, m * HT:(m + 1) * HT], oh[:, m, :], idn[0:HT, 0:HT])
                last.then_inc(onehot_pe.sem, 1)

            def hidden(p, c):
                if c == 0:
                    pe.wait_ge(*onehot_dve.at(p))
                elif c > 1:
                    pe.wait_ge(*hid_act.at(p, c - 1))
                o, cols = back_ps[:, c % 2, 0:T * SEQ], slice(c * 128, (c + 1) * 128)
                by_channels(o, lambda k, rows: w1_s[0:rows, k, cols], lambda k, rows: x2T[0:rows, k, :], False)
                nc.tensor.matmul(o, emask[:, cols], miss[:, :], start=False, stop=True).then_inc(hid_pe.sem, 1)

            def experts(p, m):
                if m == 0:
                    pe.wait_ge(*hid_act.at(p))
                o = back_ps[0:HT, m // 2, (m % 2) * D:(m % 2 + 1) * D]
                cols = slice(m * HT, (m + 1) * HT)
                for c in range(HC):
                    nc.tensor.matmul(o, hid[:, c, cols], w2_s[:, c, :], start=c == 0, stop=False)
                last = nc.tensor.matmul(o, ohT[:, cols], b2_s[:, :], start=False, stop=True)
                if m % 2:
                    last.then_inc(ffn_pe.sem, 1)

            def iteration(q, par):
                tok, front, scan, back, last = (alive(q + o) for o in (2, 1, 0, -1, -2))
                if front:
                    project(q + 1, 2)
                    project(q + 1, 3)
                if scan:
                    b_fill(q, 3, par)
                if tok:
                    tokens(q + 2, 0)
                if scan:
                    c_fill(q, 2, par)
                if last:
                    experts(q - 2, 0)
                    experts(q - 2, 1)
                    experts(q - 2, 2)
                    experts(q - 2, 3)
                if scan:
                    b_fill(q, 4, par)
                    c_fill(q, 3, par)
                if back:
                    y_transpose(q - 1, 1 - par)
                if tok:
                    tokens(q + 2, 1)
                if scan:
                    b_fill(q, 5, par)
                    c_fill(q, 4, par)
                if tok:
                    tokens(q + 2, 2)
                    tokens(q + 2, 3)
                if back:
                    x2_transpose(q - 1)
                if scan:
                    b_fill(q, 6, par)
                    c_fill(q, 5, par)
                if back:
                    logits(q - 1)
                if front:
                    bc_transpose(q + 1)
                    lnd_transpose(q + 1)
                if scan:
                    b_fill(q, 7, par)
                    c_fill(q, 6, par)
                if back:
                    onehot_transpose(q - 1)
                if front:
                    dot_fill(q + 1, 1 - par)
                    xn_transpose(q + 1)
                if back:
                    hidden(q - 1, 0)
                if scan:
                    c_fill(q, 7, par)
                if back:
                    hidden(q - 1, 1)
                if tok:
                    xr_transpose(q + 2)
                if front:
                    c_fill(q + 1, 0, 1 - par)
                if tok:
                    project(q + 2, 0)
                if front:
                    b_fill(q + 1, 0, 1 - par)
                    b_fill(q + 1, 1, 1 - par)
                if back:
                    hidden(q - 1, 2)
                if tok:
                    project(q + 2, 1)
                if back:
                    hidden(q - 1, 3)
                if front:
                    c_fill(q + 1, 1, 1 - par)
                    b_fill(q + 1, 2, 1 - par)

            for q in (-2, -1, 0, 1):
                iteration(q, q % 2)
            with pe.Fori(0, (PAIRS - 4) // 2) as i:
                iteration(i * 2 + 2, 0)
                iteration(i * 2 + 3, 1)
            for q in range(PAIRS - 2, PAIRS + 2):
                iteration(q, q % 2)

        @block.vector
        def _(dve):
            v = nc.vector
            dve.wait_ge(mixing_in.sem, MIXING_LOADS[0])
            v.memset(eps[:, 0:1], LN_EPS).then_inc(consts_set.sem, 1)
            v.memset(eps[:, 1:2], RMS_EPS).then_inc(consts_set.sem, 1)
            v.memset(eps[:, 2:3], -CLAMP_MID / CLAMP_HALF).then_inc(consts_set.sem, 1)
            v.memset(eps[:, 3:4], CLAMP_MID).then_inc(consts_set.sem, 1)
            v.memset(wp[DB:DB + 1, 1, D:W], 0.0).then_inc(consts_set.sem, 1)
            v.memset(xrT[DB:DB + 1, 1, :], 1.0).then_inc(consts_set.sem, 1)
            v.tensor_copy(idb[:, :], idn[:, :]).then_inc(consts_set.sem, 1)
            dve.wait_ge(fold_pe.sem, 1)
            v.tensor_copy(maT[:, 0:4, :], front_ps[0:RANK, 0, 0:4 * 96].rearrange("p (k n) -> p k n", k=4)) \
                .then_inc(fold_dve.sem, 1)
            v.tensor_copy(maT[:, 4:6, :], front_ps[0:RANK, 1, 0:2 * 96].rearrange("p (k n) -> p k n", k=2)) \
                .then_inc(fold_dve.sem, 1)
            dve.wait_ge(fold_pe.sem, 2)
            for k in range(MC):
                bank = back_ps[:, k // 2, :] if k < 4 else b_ps[:, 0, :]
                v.scalar_tensor_tensor(m_full[:, k, :], eyes[:, k % 2, :], md_s[:, k:k + 1],
                                       bank[0:96, (k % 2) * D:(k % 2 + 1) * D], ALU.mult, ALU.add) \
                    .then_inc(fold_dve.sem, 1)
            dve.wait_ge(weights_in.sem, SETUP_LOADS[0])
            dve.wait_ge(zeros_set.sem, ZEROS_FIRST)
            v.tensor_tensor(pos_s[:, 0, :], pos_s[:, 0, :], cls_s, ALU.add).then_inc(fold_dve.sem, 1)
            dve.wait_ge(fold_pe.sem, 3)
            for b, bank in enumerate(fold_banks):
                for rows in (slice(0, KR), slice(64, KP)):
                    v.tensor_copy(w_eff[rows, 2 * b:2 * b + 2, :],
                                  bank[rows, 0:2 * D].rearrange("p (k n) -> p k n", k=2)).then_inc(fold_dve.sem, 1)
            flat = posT.rearrange("p j k t -> p (j k t)")
            for b, bank in enumerate((back_ps[:, 0, :], back_ps[:, 1, :], b_ps[:, 0, :])):
                v.tensor_copy(flat[:, b * 4 * HT:(b + 1) * 4 * HT], bank[0:96, 0:4 * HT]).then_inc(fold_dve.sem, 1)
            v.tensor_copy(wdtT, b_ps[0:R, 1, 0:D]).then_inc(fold_dve.sem, 1)
            v.tensor_copy(encT, b_ps[0:ER, 1, D:2 * D]).then_inc(fold_dve.sem, 1)
            v.tensor_copy(encb_r, encb_s.broadcast_to([ER, HT])).then_inc(fold_dve.sem, 1)
            dve.wait_ge(fold_pe.sem, 4)
            v.tensor_copy(wp[:, 0, 0:D], front_ps[:, 0, 0:D]).then_inc(fold_dve.sem, 1)
            v.tensor_copy(wp[0:DB, 1, 0:D], front_ps[0:DB, 0, D:2 * D]).then_inc(fold_dve.sem, 1)
            v.tensor_copy(wr[:, 0, :], back_ps[:, 1, 0:E]).then_inc(fold_dve.sem, 1)
            v.tensor_copy(wr[0:DB, 1, :], back_ps[0:DB, 1, E:2 * E]).then_inc(fold_dve.sem, 1)
            v.tensor_tensor(br_t[:, :], swb_s, b_ps[0:HT, 0, 0:E], ALU.add).then_inc(fold_dve.sem, 1)
            v.tensor_copy(tok_bias[:, :, :], back_ps[0:HT, 0, 0:2 * D].rearrange("p (j d) -> p j d", j=2)) \
                .then_inc(fold_dve.sem, 1)
            v.tensor_scalar(a_bias[:, :, :], alog_s, -0.5, 0.5 * math.log(2.0), ALU.mult, ALU.add) \
                .then_inc(fold_dve.sem, 1)
            dve.wait_ge(fold_dve.sem, FOLD_ALL)
            dve.wait_ge(zeros_set.sem, ZEROS_ALL)

            def by_block(t, m):
                return t[:, m % 2, :].rearrange("p (k d) -> p k d", k=K3)

            def over_tiles(t, width):
                return t.unsqueeze(1).broadcast_to([HT, 4, width])

            def tiles(t):
                return [tile(t[:, :], m) for m in range(4)]

            def statistics(p, src, six, mv, done, base):
                for m in range(4):
                    v.bn_stats(six[:, m, :], src[m]).then_inc(done.sem, 1)
                dve.wait_ge(*done.at(p, base + 4))
                v.tensor_copy(six_count[:, :], six[:, :, 0]).then_inc(done.sem, 1)
                for m in range(4):
                    v.bn_aggr(mv[:, m, :], six[:, m, :]).then_inc(done.sem, 1)

            def tok_1(p):
                dve.wait_ge(*tokens_pe.at(p))
                made = [front_ps[0:HT, m // 2, (m % 2) * D:(m % 2 + 1) * D] for m in range(4)]
                statistics(p, made, bn6, mv1, tok_stats, 0)
                dve.wait_ge(*tok_stats.at(p, 9))
                if not first(p):
                    dve.wait_ge(*hres_ready.at(p - 1))
                for m in range(4):
                    v.scalar_tensor_tensor(tile(h_tok[:, :], m), made[m].rearrange("p (k d) -> p k d", k=K3), mv1[:, m, 0:1],
                                           by_block(lnw, m), ALU.subtract, ALU.mult).then_inc(tok_stats.sem, 1)

            def tok_2(p):
                dve.wait_ge(*tok_rstd.at(p))
                dve.wait_ge(*tok_stats.at(p))
                for m in range(4):
                    v.scalar_tensor_tensor(tile(h_tok[:, :], m), tile(h_tok[:, :], m), rs1[:, 1, m:m + 1], by_block(lnb, m),
                                           ALU.mult, ALU.add).then_inc(h_ready.sem, 1)
                dve.wait_ge(*h_ready.at(p, 4))
                statistics(p, tiles(h_tok), bn6b, mv2, h_ready, 4)
                dve.wait_ge(*h_ready.at(p, 13))
                v.tensor_scalar(neg_mean2[:, :], mv2[:, :, 0], -1.0, None, ALU.mult).then_inc(h_ready.sem, 1)

            def proj_1(p):
                dve.wait_ge(*bc_act.at(p))
                v.tensor_tensor(prod[:, :, :], bcq[:, :, 0, :], bcq[:, :, 1, :], ALU.mult).then_inc(proj_dve.sem, 1)
                dve.wait_ge(*proj_dve.at(p, 1))
                v.tensor_reduce(bcq[:, :, 2, 0:T], prod[:, :, :].rearrange("p j (t n) -> p j t n", t=T),
                                AXIS.X, ALU.add).then_inc(proj_dve.sem, 1)
                src = bcq
                for s, rest in enumerate((res1, res2, None)):
                    dve.wait_ge(*proj_dve.at(p, 2 + 2 * s))
                    v.tensor_copy(split[:, :, :, s, :], src[:, :, :, :]).then_inc(proj_dve.sem, 1)
                    if rest is not None:
                        dve.wait_ge(*proj_dve.at(p, 3 + 2 * s))
                        v.tensor_tensor(rest[:, :, :, :], src[:, :, :, :], split[:, :, :, s, :], ALU.subtract) \
                            .then_inc(proj_dve.sem, 1)
                        src = rest

            def proj_2(p):
                dve.wait_ge(*softplus_act.at(p, 9))
                v.tensor_scalar(rem[:, :], ex[:, :], 1.0, 1.0, ALU.add, ALU.subtract).then_inc(softplus_dve.sem, 1)
                dve.wait_ge(*softplus_act.at(p))
                v.tensor_tensor(sp_t[:, :], xd[:, :], lnu[:, :], ALU.add) \
                    .then_inc(softplus_dve.sem, 1)
                dve.wait_ge(*softplus_dve.at(p, 2))
                dve.wait_ge(*softplus_pool.at(p))
                v.tensor_tensor(sp_t[:, :], sp_t[:, :], rem[:, :], ALU.add).then_inc(softplus_dve.sem, 1)

            def proj_3(p):
                dve.wait_ge(*rms_act.at(p))
                for m in range(4):
                    v.scalar_tensor_tensor(tile(dn[:, :], m), tile(sp_t[:, :], m), ms[:, 2, m:m + 1],
                                           rms_t[:, :].rearrange("p (k d) -> p k d", k=K3),
                                           ALU.mult, ALU.mult).then_inc(delta_dve.sem, 1)

            def bc_copy(p, par):
                dve.wait_ge(*bc_pe.at(p))
                for k, dst in enumerate((bT, cT, qT)):
                    v.tensor_copy(dst[:, par, 1:SEG].rearrange("p (j w) -> p j w", j=2),
                                  front_bf[0:96, k * 256:k * 256 + 200].rearrange("p (j w) -> p j w", j=2)[:, :, 0:HT]) \
                        .then_inc(bc_dve.sem, 1)

            def g_make(p):
                dve.wait_ge(*lnd_act.at(p, 2))
                dve.wait_ge(*xnT_act.at(p))
                if not first(p):
                    dve.wait_ge(*v_dve.at(p - 1))
                v.tensor_tensor(gT[:, :, 1:], xnT[:, :, 1:], xnT[:, :, 0:SEQ], ALU.add).then_inc(g_dve.sem, 1)
                dve.wait_ge(*g_dve.at(p, 1))
                v.scalar_tensor_tensor(gT[:, :, 1:], sqT[:, :, :], 0.25, gT[:, :, 1:], ALU.mult, ALU.mult) \
                    .then_inc(g_dve.sem, 1)

            def dot_term(q, par):
                dve.wait_ge(*dot_pe.at(q))
                dve.wait_ge(*g_dve.at(q))
                if not (isinstance(q, int) and q < 2):
                    dve.wait_ge(*yT_pe.at(q - 2))
                v.tensor_tensor(acc[:, par, :].rearrange("p (k w) -> p k w", k=K3), gT[:, :, :],
                                b_ps[:, 0, 0:SEG].unsqueeze(1).broadcast_to([128, K3, SEG]), ALU.mult) \
                    .then_inc(acc_dve.sem, 1)

            def v_make(q, g):
                dve.wait_ge(*b_pe.at(q, g + 1))
                if not (first(q) and g < 2):
                    dve.wait_ge(*z_pool.at(q, g - 1))
                for_states = gT[:, :, :].unsqueeze(1).broadcast_to([128, 2, K3, SEG])
                for_blocks = b_ps[:, g % 2, 0:2 * SEG].rearrange("p (u w) -> p u w", u=2).unsqueeze(2) \
                    .broadcast_to([128, 2, K3, SEG])
                v.tensor_tensor(v_buf[:, g % 2, 1:].rearrange("p (u k w) -> p u k w", u=2, k=K3),
                                for_states, for_blocks, ALU.mult).then_inc(v_dve.sem, 1)

            def scan_group(q, g):
                dve.wait_ge(*z_pool.at(q, g + 1))
                dve.wait_ge(*a_act.at(q, 6 * g + 6))
                if not (first(q) and g < 2):
                    dve.wait_ge(*y_pool.at(q, 2 * (g - 1)))
                v.tensor_tensor_scan(p_buf[:, g % 2, :], z_buf[:, g % 2, :], a_ring[:, g, :], 0.0, ALU.add, ALU.mult) \
                    .then_inc(scan_dve.sem, 1)

            def c_product(q, g):
                dve.wait_ge(*c_pe.at(q, g + 1))
                dve.wait_ge(*scan_dve.at(q, g + 1))
                s = p_buf[:, g % 2, :].rearrange("p (u k w) -> p u k w", u=2, k=K3)
                for_blocks = c_ps[:, g % 2, 0:2 * SEG].rearrange("p (u w) -> p u w", u=2).unsqueeze(2) \
                    .broadcast_to([128, 2, K3, SEG])
                v.tensor_tensor(s, s, for_blocks, ALU.mult) \
                    .then_inc(p_dve.sem, 1)

            def back_1(p, par):
                dve.wait_ge(*hres_ready.at(p))
                for j in range(2):
                    dve.wait_ge(*yT_pe.at(p, j + 1))
                    cols = slice(j * T * D, (j + 1) * T * D)
                    v.tensor_tensor(h2[:, cols], hres[:, par, cols], back_ps[0:HT, j, 0:T * D], ALU.add) \
                        .then_inc(h2_dve.sem, 1)
                dve.wait_ge(*h2_dve.at(p, 2))
                statistics(p, tiles(h2), bn6c, mv3, h2_dve, 2)
                dve.wait_ge(*h2_dve.at(p, 11))
                v.tensor_scalar(neg_mean3[:, :], mv3[:, :, 0], -1.0, None, ALU.mult).then_inc(h2_dve.sem, 1)

            def back_3(p):
                s = route_dve
                dve.wait_ge(*logit_pe.at(p))
                v.tensor_tensor(lg[:, :, :].rearrange("p (t j) e -> p t j e", t=T),
                                back_ps[0:HT, :, 0:2 * E].rearrange("p t (j e) -> p t j e", j=2),
                                br_t[:, :].unsqueeze(1).unsqueeze(1).broadcast_to([HT, T, 2, E]), ALU.add).then_inc(s.sem, 1)
                dve.wait_ge(*s.at(p, 1))
                v.tensor_reduce(lmax[:, 0, :], lg[:, :, :], AXIS.X, ALU.max).then_inc(s.sem, 1)
                dve.wait_ge(*s.at(p, 2))
                v.tensor_tensor(lg[:, :, :], lg[:, :, :], lmax[:, 0, :].unsqueeze(2).broadcast_to([HT, 4, E]),
                                ALU.subtract).then_inc(s.sem, 1)
                dve.wait_ge(*s.at(p, 3))
                v.tensor_scalar(rank[:, :, :], lg[:, :, :], 0.0, None, ALU.is_equal).then_inc(s.sem, 1)
                dve.wait_ge(*s.at(p, 4))
                v.tensor_tensor(rank[:, :, :], rank[:, :, :], over_tiles(desc[:, :], E), ALU.mult).then_inc(s.sem, 1)
                dve.wait_ge(*s.at(p, 5))
                v.tensor_reduce(lmax[:, 1, :], rank[:, :, :], AXIS.X, ALU.max).then_inc(s.sem, 1)
                dve.wait_ge(*s.at(p, 6))
                v.tensor_tensor(oh[:, :, :], rank[:, :, :], lmax[:, 1, :].unsqueeze(2).broadcast_to([HT, 4, E]),
                                ALU.is_equal).then_inc(s.sem, 1)

            def back_4(p):
                dve.wait_ge(*onehot_pe.at(p))
                v.tensor_copy(ohT[:, :], back_ps[0:E, 1, 0:T * SEQ]).then_inc(onehot_dve.sem, 1)
                v.tensor_scalar(miss[:, :], back_ps[0:E, 1, 0:T * SEQ], -1.0, None, ALU.add).then_inc(onehot_dve.sem, 1)

            def back_5(p):
                s = out_dve
                dve.wait_ge(*route_act.at(p))
                v.tensor_reduce(pm[:, 0, :], er[:, :, :], AXIS.X, ALU.add).then_inc(s.sem, 1)
                dve.wait_ge(*s.at(p, 1))
                v.reciprocal(pm[:, 1, :], pm[:, 0, :]).then_inc(s.sem, 1)
                dve.wait_ge(*s.at(p, 2))
                for m in range(4):
                    if m % 2 == 0:
                        dve.wait_ge(*ffn_pe.at(p, m // 2 + 1))
                    made = back_ps[0:HT, m // 2, (m % 2) * D:(m % 2 + 1) * D].rearrange("p (k d) -> p k d", k=K3)
                    v.scalar_tensor_tensor(rows_of(o_t, m).rearrange("p (k d) -> p k d", k=K3), made, pm[:, 1, m:m + 1],
                                           tile(h2[:, :], m), ALU.mult, ALU.add).then_inc(s.sem, 1)

            def iteration(q, par):
                tok, front, scan, back, last = (alive(q + o) for o in (2, 1, 0, -1, -2))
                if scan:
                    c_product(q, 0)
                    v_make(q, 2)
                if front:
                    proj_1(q + 1)
                if scan:
                    scan_group(q, 1)
                    c_product(q, 1)
                    v_make(q, 3)
                    scan_group(q, 2)
                    c_product(q, 2)
                if front:
                    proj_2(q + 1)
                if last:
                    back_5(q - 2)
                if scan:
                    v_make(q, 4)
                    scan_group(q, 3)
                if back:
                    back_1(q - 1, 1 - par)
                if scan:
                    c_product(q, 3)
                if front:
                    proj_3(q + 1)
                if scan:
                    v_make(q, 5)
                    scan_group(q, 4)
                if tok:
                    tok_1(q + 2)
                if scan:
                    c_product(q, 4)
                if front:
                    bc_copy(q + 1, 1 - par)
                if tok:
                    tok_2(q + 2)
                if back:
                    back_3(q - 1)
                if scan:
                    v_make(q, 6)
                if back:
                    back_4(q - 1)
                if scan:
                    scan_group(q, 5)
                    c_product(q, 5)
                    v_make(q, 7)
                    scan_group(q, 6)
                    c_product(q, 6)
                if front:
                    g_make(q + 1)
                    dot_term(q + 1, 1 - par)
                    v_make(q + 1, 0)
                if scan:
                    scan_group(q, 7)
                if front:
                    v_make(q + 1, 1)
                if scan:
                    c_product(q, 7)
                if front:
                    scan_group(q + 1, 0)

            for q in (-2, -1, 0, 1):
                iteration(q, q % 2)
            with dve.Fori(0, (PAIRS - 4) // 2) as i:
                iteration(i * 2 + 2, 0)
                iteration(i * 2 + 3, 1)
            for q in range(PAIRS - 2, PAIRS + 2):
                iteration(q, q % 2)


_INS = ["x", "cls_tok", "L0_tok_conv_w", "L0_tok_class_emb", "L0_tok_pos_emb", "L0_tok_M_diag", "L0_tok_M_a",
        "L0_tok_M_b", "L0_tok_ln_w", "L0_tok_ln_b", "L0_attn_A_log", "L0_attn_D_param", "L0_attn_W_bc",
        "L0_attn_W_dt", "L0_attn_W_dtp", "L0_attn_b_dt", "L0_attn_rms_scale", "L0_ffn_enc_w", "L0_ffn_enc_b",
        "L0_ffn_sw_w", "L0_ffn_sw_b", "L0_ffn_w1", "L0_ffn_b1", "L0_ffn_w2", "L0_ffn_b2"]


def shape_constants():
    import numpy as np

    ident = np.eye(128, dtype=np.float32)
    eye_split = np.ascontiguousarray(np.eye(D, dtype=np.float32).reshape(2, 96, D).transpose(1, 0, 2))
    one, mask_bits = (np.array([f], np.float32).view(np.uint16)[1] for f in (1.0, MASK))
    pick = np.zeros((3, T, N, N, 128), np.uint16)
    dot = np.zeros((3, T * N, 128), np.uint16)
    for t in range(T):
        for n in range(N):
            pick[:, t, n, n, t * DB:(t + 1) * DB] = one
        dot[:, t, t * DB:(t + 1) * DB] = one
    mask = np.repeat(np.eye(E, dtype=np.uint16) * mask_bits, ER, axis=1)
    desc = np.tile(np.arange(E, 0, -1, dtype=np.float32), (HT, 1))
    return {"ident": ident, "eye_split": eye_split, "state_pick": pick.reshape(3 * T * N, N, 128),
            "dot_pick": dot.reshape(3 * T * N, 128), "expert_mask": mask, "rank_desc": desc}


def kernel(**inputs):
    import numpy as _np
    import concourse.bacc as _bacc
    from concourse import mybir as _mybir
    from concourse.bass_utils import run_bass_kernel_spmd as _run

    nc = _bacc.Bacc("TRN2", target_bir_lowering=False, num_devices=1)
    arrays, args = {}, []
    for name, value in [(n, inputs[n]) for n in _INS] + list(shape_constants().items()):
        a = _np.ascontiguousarray(value)
        arrays[f"in_{name}_dram"] = a
        args.append(nc.dram_tensor(f"in_{name}_dram", a.shape, _mybir.dt.from_np(a.dtype), kind="ExternalInput").ap())
    args.append(nc.dram_tensor("out_0_dram", (B, SEQ, D), FP32, kind="ExternalOutput").ap())
    build_program(nc, *args)
    r = _run(nc, [arrays], core_ids=[0])
    return r.results[0]["out_0_dram"]
```
